# Optimizing a Trainium2 kernel written in Bass

```python
import numpy as np
import jax
import jax.numpy as jnp

def _softmax(x, axis=-1):
    return jax.nn.softmax(x, axis=axis)

def _gelu(x):
    return jax.nn.gelu(x, approximate=True)

def _silu(x):
    return jax.nn.silu(x)

def _sigmoid(x):
    return jax.nn.sigmoid(x)

def _layernorm(x, axis=-1, eps=1e-05):
    m = jnp.mean(x, axis=axis, keepdims=True)
    v = jnp.var(x, axis=axis, keepdims=True)
    return (x - m) / jnp.sqrt(v + eps)

def _scatter_add(tgt, idx, src, axis=0):
    return tgt.at[idx].add(src)

def _segment_sum(src, seg, n):
    return jax.ops.segment_sum(src, seg, n)
kernel_name = 'mk_seq_preln_d1_jaxref_r8_f9361c'

def setup_inputs(seed: int=0):
    np.random.seed(seed)
    _w = jnp.asarray

    def _L0_attn_setup():
        import jax, jax.numpy as jnp
        import numpy as np
        HIDDEN = 512
        N_HEADS = 32
        N_KV_HEADS = 8
        HEAD_DIM = HIDDEN // N_HEADS
        N_REP = N_HEADS // N_KV_HEADS
        KV_DIM = N_KV_HEADS * HEAD_DIM

        def _kaiming_uniform(key, out_f, in_f):
            bound = 1.0 / np.sqrt(in_f)
            return jax.random.uniform(key, (out_f, in_f), jnp.float32, -bound, bound)

        def bitnet_linear(x, weight, scale_param):
            s = jnp.maximum(jnp.mean(jnp.abs(weight), axis=1), 1e-08)
            binary_w = jnp.sign(weight / s[:, None])
            y = jnp.einsum('bsi,oi->bso', x, binary_w)
            y = y * (s * scale_param)[None, None, :]
            return jnp.nan_to_num(y, nan=0.0, posinf=1000000.0, neginf=-1000000.0)
        key = jax.random.key(seed)
        ks = jax.random.split(key, 5)
        return {'hidden_states': jax.random.normal(ks[0], (1, 256, HIDDEN), jnp.float32), 'q_weight': _kaiming_uniform(ks[1], HIDDEN, HIDDEN), 'q_scale': jnp.ones((HIDDEN,), jnp.float32), 'k_weight': _kaiming_uniform(ks[2], KV_DIM, HIDDEN), 'k_scale': jnp.ones((KV_DIM,), jnp.float32), 'v_weight': _kaiming_uniform(ks[3], KV_DIM, HIDDEN), 'v_scale': jnp.ones((KV_DIM,), jnp.float32), 'o_weight': _kaiming_uniform(ks[4], HIDDEN, HIDDEN), 'o_scale': jnp.ones((HIDDEN,), jnp.float32)}
    _L0_attn_in = _L0_attn_setup()

    def _L0_ffn_setup():
        import jax, jax.numpy as jnp
        import numpy as np
        HID, INTER = (512, 1792)
        B, S = (2, 256)

        def _binary_diff_weight(w, base):
            d = w - base
            coeff = jnp.mean(jnp.abs(d))
            return base + coeff * jnp.sign(d)
        key = jax.random.key(seed)
        ks = jax.random.split(key, 7)
        return {'hidden_states': jax.random.normal(ks[0], (B, S, HID), dtype=jnp.float32), 'w1': jax.random.normal(ks[1], (INTER, HID), dtype=jnp.float32) * 0.02, 'mean_w1': jax.random.normal(ks[2], (INTER, HID), dtype=jnp.float32) * 0.02, 'w2': jax.random.normal(ks[3], (HID, INTER), dtype=jnp.float32) * 0.02, 'mean_w2': jax.random.normal(ks[4], (HID, INTER), dtype=jnp.float32) * 0.02, 'w3': jax.random.normal(ks[5], (INTER, HID), dtype=jnp.float32) * 0.02, 'mean_w3': jax.random.normal(ks[6], (INTER, HID), dtype=jnp.float32) * 0.02}
    _L0_ffn_in = _L0_ffn_setup()
    _d = {'L0_attn_hidden_states': _L0_attn_in['hidden_states'], 'L0_attn_q_weight': _L0_attn_in['q_weight'], 'L0_attn_q_scale': _L0_attn_in['q_scale'], 'L0_attn_k_weight': _L0_attn_in['k_weight'], 'L0_attn_k_scale': _L0_attn_in['k_scale'], 'L0_attn_v_weight': _L0_attn_in['v_weight'], 'L0_attn_v_scale': _L0_attn_in['v_scale'], 'L0_attn_o_weight': _L0_attn_in['o_weight'], 'L0_attn_o_scale': _L0_attn_in['o_scale'], 'L0_ffn_w1': _L0_ffn_in['w1'], 'L0_ffn_mean_w1': _L0_ffn_in['mean_w1'], 'L0_ffn_w2': _L0_ffn_in['w2'], 'L0_ffn_mean_w2': _L0_ffn_in['mean_w2'], 'L0_ffn_w3': _L0_ffn_in['w3'], 'L0_ffn_mean_w3': _L0_ffn_in['mean_w3']}
    _x0 = _d['L0_attn_hidden_states']
    _d['L0_attn_hidden_states'] = jax.random.normal(jax.random.fold_in(jax.random.key(seed), 1), (4, 512, 512), dtype=_x0.dtype)
    del _x0
    return _d

def reference(L0_attn_hidden_states, L0_attn_q_weight, L0_attn_q_scale, L0_attn_k_weight, L0_attn_k_scale, L0_attn_v_weight, L0_attn_v_scale, L0_attn_o_weight, L0_attn_o_scale, L0_ffn_w1, L0_ffn_mean_w1, L0_ffn_w2, L0_ffn_mean_w2, L0_ffn_w3, L0_ffn_mean_w3):

    def _L0_attn_ref(hidden_states, q_weight, q_scale, k_weight, k_scale, v_weight, v_scale, o_weight, o_scale):
        import jax, jax.numpy as jnp
        import numpy as np
        HIDDEN = 512
        N_HEADS = 32
        N_KV_HEADS = 8
        HEAD_DIM = HIDDEN // N_HEADS
        N_REP = N_HEADS // N_KV_HEADS
        KV_DIM = N_KV_HEADS * HEAD_DIM

        def _kaiming_uniform(key, out_f, in_f):
            bound = 1.0 / np.sqrt(in_f)
            return jax.random.uniform(key, (out_f, in_f), jnp.float32, -bound, bound)

        def bitnet_linear(x, weight, scale_param):
            s = jnp.maximum(jnp.mean(jnp.abs(weight), axis=1), 1e-08)
            binary_w = jnp.sign(weight / s[:, None])
            y = jnp.einsum('bsi,oi->bso', x, binary_w)
            y = y * (s * scale_param)[None, None, :]
            return jnp.nan_to_num(y, nan=0.0, posinf=1000000.0, neginf=-1000000.0)
        b, s, _ = hidden_states.shape
        q = bitnet_linear(hidden_states, q_weight, q_scale)
        k = bitnet_linear(hidden_states, k_weight, k_scale)
        v = bitnet_linear(hidden_states, v_weight, v_scale)
        q = q.reshape(b, s, N_HEADS, HEAD_DIM).transpose(0, 2, 1, 3)
        k = k.reshape(b, s, N_KV_HEADS, HEAD_DIM).transpose(0, 2, 1, 3)
        v = v.reshape(b, s, N_KV_HEADS, HEAD_DIM).transpose(0, 2, 1, 3)
        k = jnp.repeat(k, N_REP, axis=1)
        v = jnp.repeat(v, N_REP, axis=1)
        scores = jnp.einsum('bhqd,bhkd->bhqk', q, k) / np.sqrt(HEAD_DIM)
        attn = jax.nn.softmax(scores, axis=-1)
        out = jnp.einsum('bhqk,bhkd->bhqd', attn, v)
        out = out.transpose(0, 2, 1, 3).reshape(b, s, HIDDEN)
        return bitnet_linear(out, o_weight, o_scale)

    def _L0_ffn_ref(hidden_states, w1, mean_w1, w2, mean_w2, w3, mean_w3):
        import jax, jax.numpy as jnp
        import numpy as np
        HID, INTER = (512, 1792)
        B, S = (2, 256)

        def _binary_diff_weight(w, base):
            d = w - base
            coeff = jnp.mean(jnp.abs(d))
            return base + coeff * jnp.sign(d)
        W1 = _binary_diff_weight(w1, mean_w1)
        W2 = _binary_diff_weight(w2, mean_w2)
        W3 = _binary_diff_weight(w3, mean_w3)
        gate = jnp.einsum('bsh,ih->bsi', hidden_states, W1)
        up = jnp.einsum('bsh,ih->bsi', hidden_states, W3)
        h = jax.nn.silu(gate) * up
        return jnp.einsum('bsi,hi->bsh', h, W2)
    x = L0_attn_hidden_states
    x = x + _L0_attn_ref(_layernorm(x, axis=-1), L0_attn_q_weight, L0_attn_q_scale, L0_attn_k_weight, L0_attn_k_scale, L0_attn_v_weight, L0_attn_v_scale, L0_attn_o_weight, L0_attn_o_scale)
    x = x + _L0_ffn_ref(_layernorm(x, axis=-1), L0_ffn_w1, L0_ffn_mean_w1, L0_ffn_w2, L0_ffn_mean_w2, L0_ffn_w3, L0_ffn_mean_w3)
    return x

_drawn_inputs = setup_inputs


def setup_inputs(seed=0):
    import zlib

    import numpy as np

    out = dict(_drawn_inputs(seed))
    spreads = {'L0_attn_q_scale': (1.0, 0.6),
     'L0_attn_k_scale': (1.0, 0.6),
     'L0_attn_v_scale': (1.0, 0.6),
     'L0_attn_o_scale': (1.0, 0.6)}
    factors = {'L0_attn_q_weight': 8.0,
     'L0_attn_k_weight': 8.0,
     'L0_attn_v_weight': 4.312,
     'L0_attn_o_weight': 4.518,
     'L0_ffn_w1': 5.988,
     'L0_ffn_mean_w1': 7.202,
     'L0_ffn_w2': 5.87,
     'L0_ffn_mean_w2': 7.137,
     'L0_ffn_w3': 5.883,
     'L0_ffn_mean_w3': 7.153}
    for name, (base, spread) in spreads.items():
        noise = np.random.default_rng([zlib.crc32(name.encode()), seed]).standard_normal(out[name].shape)
        drawn = base * np.exp(spread * noise) if base else spread * noise
        out[name] = jnp.asarray(drawn.astype(out[name].dtype))
    for name, factor in factors.items():
        out[name] = (out[name] * factor).astype(out[name].dtype)
    return out
```

```python
import numpy as np
import concourse.bass as bass
from concourse import mybir
from contextlib import ExitStack

FP32 = mybir.dt.float32
FP32R = mybir.dt.float32r
BF16 = mybir.dt.bfloat16
I32 = mybir.dt.int32
ALU = mybir.AluOpType
ACT = mybir.ActivationFunctionType
AX = mybir.AxisListType

P = 128
BATCH, SEQ, HID = 4, 512, 512
HEADS, KV_HEADS = 32, 8
HEAD_DIM = HID // HEADS
REP = HEADS // KV_HEADS
GROUPS = BATCH * KV_HEADS
INTER = 1792
KT = HID // P
TT = SEQ // P
NT = BATCH * TT
IT = INTER // P
QT, KTILE, VTILE, OT = 0, 4, 5, 6
WTILES = 10
BIT_IN = 768
EPS = 1e-5
FLT_MAX = float(np.finfo(np.float32).max)
GUARD = 1e6
SHIFT_MAX = 3e38
STACK = 96
SHIFT_ROW = 64


def positive(eng, sem, value):
    if not isinstance(value, int) or value > 0:
        eng.wait_ge(sem, value)


def settle(eng):
    eng.nop(nofuse=True)


class Chain:

    def __init__(self, eng, sem):
        self.eng, self.sem, self.base, self.k, self.saved = eng, sem, 0, 0, 0

    def link(self, ins):
        ins.then_inc(self.sem, 1)
        self.k += 1
        self.eng.wait_ge(self.sem, self.base + self.k)

    def enter(self, i, per):
        self.saved, self.per = self.base + self.k, per
        self.base, self.k = self.saved + i * per, 0

    def leave(self, times):
        assert self.k == self.per, (self.k, self.per)
        self.base, self.k = self.saved + times * self.per, 0


def decoder_layer(nc, x, q_w, q_s, k_w, k_s, v_w, v_s, o_w, o_s, w1, m1, w2, m2, w3, m3, out):
    ctx = ExitStack()

    def sem(name):
        return ctx.enter_context(nc.semaphore(name))

    def sems(name, n):
        return [sem(f"{name}{i}") for i in range(n)]

    def region(scope):
        return lambda name, shape, dt=FP32: scope.enter_context(nc.sbuf_tensor(name, shape, dt))

    q_dram = nc.dram_tensor("q_parts", [GROUPS, 2, HEAD_DIM, REP, SEQ], FP32, kind="Internal").ap()
    k_dram = nc.dram_tensor("k_stack", [GROUPS, 4 * HEAD_DIM, SEQ], FP32, kind="Internal").ap()
    fac_dram = nc.dram_tensor("factors", [2, WTILES, P], FP32, kind="Internal").ap()
    att_dram = nc.dram_tensor("attended", [GROUPS // 4, TT, P, 4 * 64], FP32, kind="Internal").ap()
    x1_dram = nc.dram_tensor("residual", [NT, P, HID], FP32, kind="Internal").ap()

    keep = region(ctx)
    ident = keep("ident", [P, P])
    ident16 = keep("ident16", [P, P], BF16)
    half = keep("minus_half", [P, NT])
    ones = keep("ones", [P, P])
    x2T = keep("x2T", [P, NT, SEQ])
    until_c = ExitStack()
    mid = region(until_c)
    signs_o = mid("signs_o", [P, KT, HID], FP32R)
    fac_row = mid("fac_row", [P, 2, WTILES, P])
    x_sb = mid("x_sb", [P, NT, HID])
    v_sb = mid("v_sb", [P, GROUPS, TT, HEAD_DIM])

    with ExitStack() as scope:
        sb = region(scope)
        w_nat = sb("w_nat", [P, WTILES, HID])
        w_sgn = sb("w_sgn", [P, WTILES, HID], BF16)
        signs = sb("signs_qkv", [P, KT, BIT_IN], FP32R)
        scl = sb("scl", [P, WTILES])
        wstat = sb("wstat", [P, 6, WTILES])
        stats = sb("stats", [P, NT, 6])
        mv = sb("mv", [P, NT, 2])
        ve = sb("ve", [P, NT])
        rstd = sb("rstd", [P, NT])
        xn = [x2T[:, TT * p:TT * p + TT, :] for p in range(2)]
        xh = [sb(f"xh{p}", [P, KT, SEQ], FP32R) for p in range(2)]
        xl = [sb(f"xl{p}", [P, KT, SEQ], FP32R) for p in range(2)]
        yq = [w_nat[:, 5 * p:5 * p + 5, :] for p in range(2)]
        q_hi = sb("q_hi", [P, 5, SEQ], FP32R)
        q_lo = sb("q_lo", [P, 5, SEQ], FP32R)
        g_mask = sb("g_mask", [P, SEQ], I32)
        g_alt = sb("g_alt", [P, SEQ])
        vy = x2T[:, 2 * TT, :].rearrange("p (t c) -> p t c", c=P)
        vz = sb("vz", [P, TT, P])
    with ExitStack() as scope:
        sb = region(scope)
        q_slot = [sb(f"q_slot{s}", [STACK, REP, SEQ], FP32R) for s in range(4)]
        k_slot = [sb(f"k_slot{s}", [STACK, SEQ], FP32R) for s in range(4)]
        v_slot = [sb(f"v_slot{s}", [P, TT, 32]) for s in range(2)]
        probs = [sb(f"probs{s}", [P, REP, SEQ]) for s in range(2)]
        nmx = [sb(f"nmx{s}", [P, REP * TT]) for s in range(2)]
        shift = [sb(f"shift{s}", [REP * TT, 2, P], FP32R) for s in range(2)]
        u_sb = sb("u_sb", [P, SEQ])
        u_rec = sb("u_rec", [P, REP * TT])
        att = [sb(f"att{s}", [P, TT, 64]) for s in range(2)]
    with ExitStack() as scope:
        sb = region(scope)
        an = [sb(f"an{p}", [P, TT, HID]) for p in range(1)]
        ah = [sb(f"ah{p}", [P, KT, SEQ], FP32R) for p in range(1)]
        al = [sb(f"al{p}", [P, KT, SEQ], FP32R) for p in range(1)]
        oy = [sb(f"oy{p}", [P, SEQ]) for p in range(1)]
        o_mask = sb("o_mask", [P, SEQ], I32)
        o_alt = sb("o_alt", [P, SEQ])
        oz = sb("oz", [P, SEQ])
        x1 = sb("x1", [P, TT, HID])
        st2 = sb("st2", [P, TT, 6])
        mv2 = sb("mv2", [P, TT, 2])
        ve2 = sb("ve2", [P, TT])
        rstd2 = sb("rstd2", [P, TT])
        xn2 = sb("xn2", [P, TT, HID])
    until_c.close()
    late = region(ctx)
    w1T = late("w1T", [P, IT, HID])
    w3T = late("w3T", [P, IT, HID])
    w2T = late("w2T", [P, IT, HID])
    with ExitStack() as scope:
        sb = region(scope)
        wn = [sb(f"wn{p}", [P, 3, HID]) for p in range(2)]
        mn = [sb(f"mn{p}", [P, 3, HID]) for p in range(2)]
        sg = [sb(f"sg{p}", [P, 3, HID]) for p in range(2)]
        dsum = sb("dsum", [P, 3, IT])
        dtot = sb("dtot", [P, 3])
        coeff = sb("coeff", [P, 3])
    with ExitStack() as scope:
        sb = region(scope)
        wh = [sb(f"wh{p}", [P, 3, HID], FP32R) for p in range(2)]
        wl = [sb(f"wl{p}", [P, 3, HID], FP32R) for p in range(2)]
        fxh = sb("fxh", [P, KT, SEQ], FP32R)
        fxl = sb("fxl", [P, KT, SEQ], FP32R)
        gate = [sb(f"gate{p}", [P, SEQ]) for p in range(2)]
        hid = [sb(f"hid{p}", [P, SEQ]) for p in range(2)]
        hh = [sb(f"hh{p}", [P, SEQ], FP32R) for p in range(2)]
        hl = [sb(f"hl{p}", [P, SEQ], FP32R) for p in range(2)]
        x1r = sb("x1r", [P, TT, HID])
        ob = [sb(f"ob{p}", [P, HID]) for p in range(2)]

    psum = ctx.enter_context(nc.psum_tensor("psum", [P, 8, 512], FP32))
    BANK = [psum[:, i, :] for i in range(8)]

    x_in = sems("x_in", BATCH)
    w_in = sems("w_in", 3)
    scl_in = sem("scl_in")
    const_ok = sem("const_ok")
    wstat_ok = sem("wstat_ok")
    sgn_ok = sem("sgn_ok")
    sgnT_ok = sem("sgnT_ok")
    signs_ok = sem("signs_ok")
    fac_out = sem("fac_out")
    fac_in = sem("fac_in")
    stat_ch = sem("stat_ch")
    rstd_ok = sem("rstd_ok")
    dve_ch = sem("dve_ch")
    xn_ok = sems("xn_ok", 2)
    xT_ok = sems("xT_ok", 2)
    xh_ok = sems("xh_ok", 2)
    xl_ok = sems("xl_ok", 2)
    q_mm = sem("q_mm")
    yq_ok = sem("yq_ok")
    yg_ok = sem("yg_ok")
    qh_ok = sem("qh_ok")
    ql_ok = sem("ql_ok")
    part_out = sems("part_out", 5)
    v_mm = sems("v_mm", 2)
    vy_ok = sem("vy_ok")
    v_ok = sem("v_ok")

    def w_source(m):
        return {0: q_w, 1: q_w, 2: q_w, 3: q_w, 4: k_w, 5: v_w}.get(m, o_w)

    slot_in = sems("slot_in", 4)
    cleared = sem("cleared")
    slot_init = sem("slot_init")
    vs_ok = sem("vs_ok")
    s_mm = sem("s_mm")
    s_max = sem("s_max")
    mT_ok = sem("mT_ok")
    sh_hi = sem("sh_hi")
    sh_lo = sem("sh_lo")
    shift_in = sems("shift_in", 4)
    t_mm = sem("t_mm")
    exp_ok = sem("exp_ok")
    pv_mm = sem("pv_mm")
    u_ok = sem("u_ok")
    uT_ok = sem("uT_ok")
    rec_ok = sem("rec_ok")
    att_ok = sem("att_ok")
    att_out = sems("att_out", 2)

    an_in = sem("an_in")
    aT_ok = sem("aT_ok")
    ah_ok = sem("ah_ok")
    al_ok = sem("al_ok")
    o_mm = sem("o_mm")
    oy_ok = sem("oy_ok")
    x1_ok = sem("x1_ok")
    x1_out = sem("x1_out")
    ve2_ok = sem("ve2_ok")
    rstd2_ok = sem("rstd2_ok")
    xn2_ok = sem("xn2_ok")
    x2T_mm = sem("x2T_mm")
    x2T_ok = sem("x2T_ok")
    c_ch = sem("c_ch")
    wn_in = sems("wn_in", 2)
    d_ok = sems("d_ok", 2)
    dtot_ok = sem("dtot_ok")
    ctot_mm = sem("ctot_mm")
    coeff_ok = sem("coeff_ok")
    sg_ok = sems("sg_ok", 2)
    tile_done = sems("tile_done", 2)
    wT_mm = sems("wT_mm", 2)
    wT_ok = sems("wT_ok", 2)
    fxh_ok = sem("fxh_ok")
    fxl_ok = sem("fxl_ok")
    wh_a = sems("wh_a", 2)
    wh_p = sems("wh_p", 2)
    wl_ok = sems("wl_ok", 2)
    g_mm = sems("g_mm", 2)
    u_mm = sems("u_mm", 2)
    silu_ok = sems("silu_ok", 2)
    h_ok = sems("h_ok", 2)
    hh_ok = sems("hh_ok", 2)
    hl_ok = sems("hl_ok", 2)
    d_mm = sems("d_mm", 2)
    x1r_in = sem("x1r_in")
    ob_ok = sem("ob_ok")
    out_done = sems("out_done", 2)

    LAST_G = GROUPS - 1
    S_AHEAD = 14
    S_USES = GROUPS * 8

    block = ctx.enter_context(nc.Block())

    @block.sync
    def _(sp):
        for b in range(BATCH):
            sp.dma_start(x_sb[:, b * TT:(b + 1) * TT, :],
                         x[b].rearrange("(t p) c -> p t c", p=P)).then_inc(x_in[b], 16)
        sp.wait_ge(wstat_ok, 3)
        sp.dma_start(fac_dram.rearrange("a w p -> p a w"), wstat[:, 3:5, :],
                     allow_slow_non_contiguous=True).then_inc(fac_out, 16)
        sp.wait_ge(fac_out, 16)
        sp.dma_start(fac_row[:].rearrange("p a w c -> p (a w c)"),
                     fac_dram.rearrange("a w p -> (a w p)").unsqueeze(0).to_broadcast([P, 2 * WTILES * P])
                     ).then_inc(fac_in, 16)

        with sp.Fori(0, 2) as i:
            for p in range(2):
                b = 2 * i + p
                for m in range(5):
                    for part, (src, ready) in enumerate(((q_hi, qh_ok), (q_lo, ql_ok))):
                        sp.wait_ge(ready, 5 * b + m + 1)
                        if m < 4:
                            for half_tile in range(2):
                                g = 8 * b + 2 * m + half_tile
                                dst = q_dram[bass.ds(g, 1), part].rearrange("o d j t -> (o j) d t")
                                rows = src[64 * half_tile:64 * half_tile + 64, m, :].bitcast(FP32)
                                sp.dma_start(dst, rows).then_inc(part_out[m], 16)
                        else:
                            for copy in range(2):
                                r = (2 * part + copy) * HEAD_DIM
                                dst = k_dram[bass.ds(8 * b, 8), r:r + HEAD_DIM, :]
                                sp.dma_start(dst, src[:, m, :].bitcast(FP32)).then_inc(part_out[m], 16)

        for m in range(5):
            sp.wait_ge(part_out[m], BATCH * 64)
        sp.wait_ge(v_ok, BATCH)
        sp.wait_ge(slot_init, 14)

        def load_group(g, s):
            for copy in range(2):
                sp.dma_start(q_slot[s][32 * copy:32 * copy + 32].bitcast(FP32),
                             q_dram[bass.ds(g, 1)].rearrange("o l d j t -> (o l d) j t")
                             ).then_inc(slot_in[s], 16)
            sp.dma_start(k_slot[s][0:SHIFT_ROW].bitcast(FP32),
                         k_dram[bass.ds(g, 1)].rearrange("o r t -> (o r) t")).then_inc(slot_in[s], 16)

        def load_shift(g, s):
            for part, ready in enumerate((sh_hi, sh_lo)):
                sp.wait_ge(ready, g + 1)
                sp.dma_start(q_slot[s][SHIFT_ROW + part:SHIFT_ROW + part + 1].bitcast(FP32).rearrange("o j (t c) -> o (j t) c", c=P),
                             shift[s % 2][:, part, :].bitcast(FP32)).then_inc(shift_in[s], 16)

        def store_att(i, s):
            sp.wait_ge(att_ok, 4 * i + s + 1)
            sp.dma_start(att_dram[bass.ds(i, 1), :, :, 64 * s:64 * s + 64].rearrange("o t p c -> (o p) t c"),
                         att[s % 2][:]).then_inc(att_out[s % 2], 16)

        for g in range(3):
            load_group(g, g)
        load_shift(0, 0)

        def sp_steps(i, first=False, last=False):
            for s in range(4):
                g = 4 * i + s
                if not (last and s > 0):
                    positive(sp, t_mm, 16 * g)
                    load_group(g + 3, (s + 3) % 4)
                if not (last and s == 3):
                    load_shift(g + 1, (s + 1) % 4)
                if not (first and s == 0):
                    store_att(*((i, s - 1) if s else (i - 1, 3)))

        sp_steps(0, first=True)
        with sp.Fori(1, GROUPS // 4 - 1) as i:
            sp_steps(i)
        sp_steps(GROUPS // 4 - 1, last=True)
        store_att(GROUPS // 4 - 1, 3)
        for s in range(2):
            sp.wait_ge(att_out[s], 16 * GROUPS // 2)

        with sp.Fori(0, BATCH) as b:
            sp.wait_ge(aT_ok, 4 * b)
            for part in range(2):
                sp.dma_start(an[0][:, :, 256 * part:256 * part + 256],
                             att_dram[bass.ds(2 * b + part, 1)].rearrange("o t p c -> (o p) t c")).then_inc(an_in, 16)
            sp.wait_ge(x1_ok, 4 * (b + 1))
            sp.dma_start(x1_dram[bass.ds(4 * b, 4)].rearrange("t p c -> p t c"), x1[:]).then_inc(x1_out, 16)

        sp.wait_ge(x2T_ok, NT)
        sp.wait_ge(x1_out, 16 * BATCH)
        with sp.Fori(0, 2) as lap:
            with sp.Fori(0, IT // 2) as i:
                for p in range(2):
                    e = 2 * i + p
                    sp.wait_ge(tile_done[p], 3 * (lap * (IT // 2) + i))
                    for k, (w, m) in enumerate(((w1, m1), (w3, m3))):
                        sp.dma_start(wn[p][:, k, :], w[bass.ds(e * P, P), :]).then_inc(wn_in[p], 16)
                        sp.dma_start(mn[p][:, k, :], m[bass.ds(e * P, P), :]).then_inc(wn_in[p], 16)
                    for w, dst in ((w2, wn), (m2, mn)):
                        sp.dma_start(dst[p][:, 2, :].rearrange("p (t c) -> p t c", c=P),
                                     w[:, bass.ds(e * P, P)].rearrange("(t p) c -> p t c", p=P)
                                     ).then_inc(wn_in[p], 16)

        with sp.Fori(0, BATCH) as b:
            sp.wait_ge(ob_ok, 4 * b)
            sp.dma_start(x1r[:], x1_dram[bass.ds(4 * b, 4)].rearrange("t p c -> p t c")).then_inc(x1r_in, 16)
            for t in range(TT):
                sp.wait_ge(ob_ok, 4 * b + t + 1)
                sp.dma_start(out[bass.ds(b, 1), t * P:(t + 1) * P, :].rearrange("o p c -> (o p) c"),
                             ob[t % 2][:]).then_inc(out_done[t % 2], 16)
        for p in range(2):
            sp.wait_ge(out_done[p], 16 * NT // 2)


    @block.gpsimd
    def _(pool):
        nc.gpsimd.memset(ident[:], 0.0).then_inc(const_ok, 1)
        pool.wait_ge(const_ok, 1)
        nc.gpsimd.affine_select(out=ident[:], in_=ident[:], compare_op=ALU.not_equal, fill=1.0, base=0,
                                pattern=[[-1, P]], channel_multiplier=1).then_inc(const_ok, 1)
        pool.wait_ge(const_ok, 2)
        nc.gpsimd.tensor_copy(ident16[:], ident[:]).then_inc(const_ok, 1)
        nc.gpsimd.memset(half[:], -0.5).then_inc(const_ok, 1)
        nc.gpsimd.memset(ones[:], 1.0).then_inc(const_ok, 1)
        pool.wait_ge(const_ok, 5)
        pool.wait_ge(stat_ch, 2 * NT + 1)
        nc.gpsimd.tensor_tensor(rstd[:], ve[:], half[:], ALU.pow).then_inc(rstd_ok, 1)

        with pool.Fori(0, 2) as i:
            for p in range(2):
                b = 2 * i + p
                for m in range(5):
                    pool.wait_ge(yg_ok, 5 * b + m + 1)
                    pool.wait_ge(part_out[m], 64 * b)
                    settle(pool)
                    nc.gpsimd.tensor_copy(q_hi[:, m, :], g_alt[:]).then_inc(qh_ok, 1)

        pool.wait_ge(v_ok, BATCH)
        for m in range(5):
            pool.wait_ge(part_out[m], BATCH * 64)
        for s in range(4):
            nc.gpsimd.memset(q_slot[s][SHIFT_ROW:STACK].bitcast(FP32), 0.0).then_inc(slot_init, 1)

        def clear_shift(g, s):
            settle(pool)
            nc.gpsimd.memset(q_slot[s][SHIFT_ROW:SHIFT_ROW + 2].bitcast(FP32), 0.0).then_inc(cleared, 1)

        def fill_values(g, s):
            settle(pool)
            nc.gpsimd.tensor_copy(v_slot[s][:, :, 0:HEAD_DIM],
                                  v_sb[:, bass.ds(g, 1), :, :].rearrange("p o t d -> p (o t) d")).then_inc(vs_ok, 1)

        pool.wait_ge(slot_init, 14)
        fill_values(0, 0)
        fill_values(1, 1)

        def pool_steps(base, first=False, last=False):
            for s in range(4):
                g = base + s
                if not (first and s == 0):
                    if not (last and s > 0):
                        pool.wait_ge(t_mm, 16 * g)
                        pool.wait_ge(vs_ok, g + 1)
                        clear_shift(g + 3, (s + 3) % 4)
                    if not (last and s == 3):
                        pool.wait_ge(pv_mm, 4 * g)
                        if not (last and s > 0):
                            pool.wait_ge(cleared, g)
                        fill_values(g + 1, (s + 1) % 2)

        pool_steps(0, first=True)
        with pool.Fori(1, GROUPS // 4 - 1) as i:
            pool_steps(4 * i)
        pool_steps(GROUPS - 4, last=True)

        with pool.Fori(0, BATCH) as b:
            pool.wait_ge(ve2_ok, b + 1)
            nc.gpsimd.tensor_tensor(rstd2[:], ve2[:], half[:, 0:TT], ALU.pow).then_inc(rstd2_ok, 1)
        with pool.Fori(0, 2) as lap:
            with pool.Fori(0, IT // 2) as i:
                for p in range(2):
                    use = lap * (IT // 2) + i
                    pool.wait_ge(wn_in[p], 96 * (use + 1))
                    nc.gpsimd.tensor_tensor(wn[p][:], wn[p][:], mn[p][:], ALU.subtract).then_inc(d_ok[p], 1)
        with pool.Fori(0, BATCH) as b:
            with pool.Fori(0, IT // 2) as i:
                for p in range(2):
                    use = (IT // 2) * b + i
                    pool.wait_ge(d_mm[p], use)
                    pool.wait_ge(wT_ok[0], 3 * (IT // 2))
                    pool.wait_ge(wT_ok[1], 3 * (IT // 2))
                    settle(pool)
                    nc.gpsimd.tensor_copy(wh[p][:, 2, :], w2T[:, bass.ds(2 * i + p, 1), :].rearrange("p o c -> p (o c)")
                                          ).then_inc(wh_p[p], 1)

    @block.scalar
    def _(act):
        for n, (src, t0, tiles) in enumerate(((q_w, QT, 4), (k_w, KTILE, 1), (v_w, VTILE, 1), (o_w, OT, 4))):
            act.dma_start(w_nat[:, t0:t0 + tiles, :], src.rearrange("(t p) c -> p t c", p=P)
                          ).then_inc(w_in[(0, 1, 1, 2)[n]], 16)
        for src, t0, tiles in ((q_s, QT, 4), (k_s, KTILE, 1), (v_s, VTILE, 1), (o_s, OT, 4)):
            act.dma_start(scl[:, t0:t0 + tiles], src.rearrange("(t p) -> p t", p=P),
                          allow_slow_non_contiguous=True).then_inc(scl_in, 16)
        act.wait_ge(wstat_ok, 1)
        for m in range(WTILES):
            nc.scalar.activation(w_sgn[:, m, :], w_nat[:, m, :], ACT.Sign,
                                 scale=wstat[:, 2, m:m + 1]).then_inc(sgn_ok, 1)
        act.wait_ge(wstat_ok, 3)

        with act.Fori(0, 2) as i:
            for p in range(2):
                b = 2 * i + p
                for kt in range(KT):
                    act.wait_ge(xT_ok[p], 4 * i + kt + 1)
                    if kt == 0:
                        act.wait_ge(v_mm[p], i)
                    nc.scalar.activation(xh[p][:, kt, :], BANK[kt], ACT.Copy).then_inc(xh_ok[p], 1)
            for p in range(2):
                b = 2 * i + p
                for m in range(5):
                    act.wait_ge(q_mm, 5 * b + m + 1)
                    if m == 0:
                        act.wait_ge(ql_ok, 5 * (2 * i))
                    nc.scalar.activation(yq[p][:, m, :], BANK[4 + m % 3], ACT.Copy,
                                         scale=wstat[:, 3, m:m + 1]).then_inc(yq_ok, 1)

        act.wait_ge(v_ok, BATCH)

        def act_steps(base, first=False, last=False):
            for s in range(4):
                g = base + s
                for kt in range(TT):
                    for j in range(REP):
                        act.wait_ge(t_mm, 16 * g + 4 * kt + j + 1)
                        if j == 0:
                            positive(act, pv_mm, 4 * g + kt - 1)
                        nc.scalar.activation(probs[kt % 2][:, j, :], BANK[4 + j % 2], ACT.Exp,
                                             scale=HEAD_DIM ** -0.5).then_inc(exp_ok, 1)
                        if kt == 1 and j == 0 and not (first and s == 0):
                            copy_u(g - 1)

        def copy_u(g):
            act.wait_ge(pv_mm, 4 * g + 4)
            positive(act, uT_ok, g)
            nc.scalar.activation(u_sb[:], BANK[6], ACT.Copy).then_inc(u_ok, 1)

        act_steps(0, first=True)
        with act.Fori(1, GROUPS // 4 - 1) as i:
            act_steps(4 * i)
        act_steps(GROUPS - 4, last=True)
        copy_u(LAST_G)

        act.wait_ge(att_out[0], 16 * GROUPS // 2)
        act.wait_ge(att_out[1], 16 * GROUPS // 2)
        with act.Fori(0, BATCH) as b:
            for kt in range(KT):
                act.wait_ge(aT_ok, 4 * b + kt + 1)
                act.wait_ge(o_mm, 4 * b)
                nc.scalar.activation(ah[0][:, kt, :], BANK[kt], ACT.Copy).then_inc(ah_ok, 1)
            for kt in range(KT):
                act.wait_ge(x2T_mm, 4 * b + kt + 1)
                nc.scalar.activation(x2T[:, bass.ds(4 * b + kt, 1), :].rearrange("p o c -> p (o c)"), BANK[kt],
                                     ACT.Copy).then_inc(x2T_ok, 1)
        with act.Fori(0, IT // 2) as i:
            for p in range(2):
                act.wait_ge(d_ok[p], IT // 2 + i + 1)
                act.wait_ge(wT_mm[p], 3 * i)
                nc.scalar.activation(sg[p][:], wn[p][:], ACT.Sign).then_inc(sg_ok[p], 1)
            for p in range(2):
                for k, dst in enumerate((w1T, w3T, w2T)):
                    act.wait_ge(wT_mm[p], 3 * i + k + 1)
                    nc.scalar.activation(dst[:, bass.ds(2 * i + p, 1), :].rearrange("p o c -> p (o c)"),
                                         BANK[3 * p + k], ACT.Copy).then_inc(wT_ok[p], 1)
        with act.Fori(0, BATCH) as b:
            for kt in range(KT):
                act.wait_ge(u_mm[0], (IT // 2) * b)
                act.wait_ge(u_mm[1], (IT // 2) * b)
                nc.scalar.activation(fxh[:, kt, :], x2T[:, bass.ds(4 * b + kt, 1), :].rearrange("p o c -> p (o c)"),
                                     ACT.Copy).then_inc(fxh_ok, 1)
            with act.Fori(0, IT // 2) as i:
                for p in range(2):
                    use = (IT // 2) * b + i
                    act.wait_ge(d_mm[p], use)
                    for k, src in enumerate((w1T, w3T)):
                        nc.scalar.activation(wh[p][:, k, :], src[:, bass.ds(2 * i + p, 1), :].rearrange("p o c -> p (o c)"),
                                             ACT.Copy).then_inc(wh_a[p], 1)
                    act.wait_ge(g_mm[p], use + 1)
                    act.wait_ge(h_ok[p], use)
                    nc.scalar.activation(gate[p][:], BANK[p], ACT.Silu).then_inc(silu_ok[p], 1)
                    act.wait_ge(h_ok[p], use + 1)
                    nc.scalar.activation(hh[p][:], hid[p][:], ACT.Copy).then_inc(hh_ok[p], 1)

    @block.vector
    def _(dve):
        v = nc.vector
        chain = Chain(dve, dve_ch)

        for n, (t0, tiles) in enumerate(((QT, 4), (KTILE, 2), (OT, 4))):
            dve.wait_ge(w_in[n], (16, 32, 16)[n])
            chain.link(v.tensor_reduce(wstat[:, 0, t0:t0 + tiles], w_nat[:, t0:t0 + tiles, :], AX.X, ALU.add,
                                       apply_absolute_value=True))
        chain.link(v.tensor_scalar(wstat[:, 1, :], wstat[:, 0, :], 1.0 / HID, 1e-8, ALU.mult, ALU.max))
        v.reciprocal(wstat[:, 2, :], wstat[:, 1, :]).then_inc(wstat_ok, 1)
        dve.wait_ge(scl_in, 64)
        chain.link(v.tensor_tensor(wstat[:, 5, :], wstat[:, 1, :], scl[:], ALU.mult))
        v.tensor_scalar(wstat[:, 3, :], wstat[:, 5, :], -FLT_MAX, FLT_MAX, ALU.max, ALU.min).then_inc(wstat_ok, 1)
        chain.link(v.tensor_scalar(wstat[:, 0, :], wstat[:, 5, :], 0.0, 0.0, ALU.mult, ALU.is_equal))
        v.tensor_scalar(wstat[:, 4, :], wstat[:, 0, :], -1.0, 1.0, ALU.mult, ALU.add).then_inc(wstat_ok, 1)

        for t in range(NT):
            dve.wait_ge(x_in[t // TT], 16)
            v.bn_stats(stats[:, t, :], x_sb[:, t, :]).then_inc(stat_ch, 1)
        for t in range(NT):
            dve.wait_ge(stat_ch, NT)
            v.bn_aggr(mv[:, t, :], stats[:, t, :]).then_inc(stat_ch, 1)
        dve.wait_ge(stat_ch, 2 * NT)
        v.tensor_scalar(ve[:], mv[:, :, 1], EPS, None, ALU.add).then_inc(stat_ch, 1)

        for m in range(WTILES):
            dve.wait_ge(sgnT_ok, m + 1)
            dst = signs[:, :, m * P:(m + 1) * P] if m < OT else signs_o[:, :, (m - OT) * P:(m - OT + 1) * P]
            src = BANK[m % 4].bitcast(BF16)[:, 0:HID].rearrange("p (t c) -> p t c", c=P)
            v.tensor_copy(dst, src).then_inc(signs_ok, 1)
        dve.wait_ge(rstd_ok, 1)
        dve.wait_ge(fac_in, 16)

        def norm(i, p):
            for t in range(TT):
                tile = 4 * (2 * i + p) + t
                dve.wait_ge(xT_ok[p], 4 * i)
                v.tensor_scalar(xn[p][:, t, :], x_sb[:, bass.ds(tile, 1), :].rearrange("p o c -> p (o c)"),
                                mv[:, bass.ds(tile, 1), 0:1].rearrange("p o c -> p (o c)"),
                                rstd[:, bass.ds(tile, 1)], ALU.subtract, ALU.mult).then_inc(xn_ok[p], 1)

        with dve.Fori(0, 2) as i:
            chain.enter(i, 2 * (5 + 3))
            for p in range(2):
                norm(i, p)
            for p in range(2):
                for kt in range(KT):
                    dve.wait_ge(xh_ok[p], 4 * i + kt + 1)
                    v.tensor_tensor(xl[p][:, kt, :], BANK[kt], xh[p][:, kt, :].bitcast(FP32),
                                    ALU.subtract).then_inc(xl_ok[p], 1)
            for p in range(2):
                b = 2 * i + p
                for m in range(5):
                    y = yq[p][:, m, :]
                    dve.wait_ge(yq_ok, 5 * b + m + 1)
                    dve.wait_ge(ql_ok, 5 * b + m)
                    if m == 0:
                        dve.wait_ge(v_ok, b)
                    v.tensor_scalar(g_alt[:], y, GUARD, -GUARD, ALU.min, ALU.max)
                    chain.link(v.tensor_scalar(g_mask[:], y, wstat[:, 4, m:m + 1], 0.0, ALU.mult, ALU.is_equal))
                    settle(dve)
                    v.copy_predicated(g_alt[:], g_mask[:], y).then_inc(yg_ok, 1)
                    dve.wait_ge(qh_ok, 5 * b + m + 1)
                    v.tensor_tensor(q_lo[:, m, :], g_alt[:], q_hi[:, m, :].bitcast(FP32), ALU.subtract).then_inc(ql_ok, 1)
                row = [fac_row[:, a, VTILE, :].unsqueeze(1).to_broadcast([P, TT, P]) for a in range(2)]
                alt = g_alt[:].rearrange("p (t c) -> p t c", c=P)
                mask = g_mask[:].rearrange("p (t c) -> p t c", c=P)
                dve.wait_ge(v_mm[p], i + 1)
                v.tensor_tensor(vy, BANK[7].rearrange("p (t c) -> p t c", c=P), row[0], ALU.mult).then_inc(vy_ok, 1)
                dve.wait_ge(vy_ok, b + 1)
                dve.wait_ge(ql_ok, 5 * (b + 1))
                v.tensor_scalar(alt, vy, GUARD, -GUARD, ALU.min, ALU.max)
                chain.link(v.tensor_tensor(vz[:], vy, row[1], ALU.mult))
                chain.link(v.tensor_scalar(mask, vz[:], 0.0, None, ALU.is_equal))
                settle(dve)
                chain.link(v.copy_predicated(alt, mask, vy))
                for kv in range(KV_HEADS):
                    last = v.tensor_copy(v_sb[:, bass.ds(8 * b + kv, 1), :, :].rearrange("p o t d -> p (o t) d"),
                                         alt[:, :, kv * HEAD_DIM:(kv + 1) * HEAD_DIM])
                last.then_inc(v_ok, 1)
            chain.leave(2)

        for m in range(5):
            dve.wait_ge(part_out[m], BATCH * 64)
        for s in range(4):
            v.memset(k_slot[s][SHIFT_ROW:STACK].bitcast(FP32), 0.0).then_inc(slot_init, 1)
        dve.wait_ge(slot_init, 8)
        for s in range(4):
            v.memset(k_slot[s][SHIFT_ROW:SHIFT_ROW + 2].bitcast(FP32), 1.0).then_inc(slot_init, 1)
        for s in range(2):
            v.memset(v_slot[s][:, :, HEAD_DIM:], 1.0).then_inc(slot_init, 1)

        def maxima(base, nn):
            rel, j, half_tile = nn // 8, nn % 8 // 2, nn % 2
            c = j * TT + 2 * half_tile
            dve.wait_ge(s_mm, 8 * base + nn + 1)
            pair = psum[:, 2 * half_tile:2 * half_tile + 2, :]
            v.tensor_reduce(nmx[rel % 2][:, c:c + 2], pair, AX.X, ALU.max, negate=True).then_inc(s_max, 1)

        def split_shift(g, s, reused):
            dve.wait_ge(mT_ok, g + 1)
            if reused is not None:
                dve.wait_ge(shift_in[(s + 2) % 4], reused)
            src = BANK[7][0:REP * TT, 0:P]
            v.tensor_scalar(shift[s % 2][:, 0, :], src, -SHIFT_MAX, SHIFT_MAX, ALU.max, ALU.min).then_inc(sh_hi, 1)
            dve.wait_ge(sh_hi, g + 1)
            v.scalar_tensor_tensor(shift[s % 2][:, 1, :], src, -SHIFT_MAX, shift[s % 2][:, 0, :].bitcast(FP32),
                                   ALU.max, ALU.subtract).then_inc(sh_lo, 1)

        def normalise(g, s, reused):
            u = BANK[7].rearrange("p (n c) -> p n c", c=32)
            dve.wait_ge(uT_ok, g + 1)
            v.reciprocal(u_rec[:], u[:, :, HEAD_DIM]).then_inc(rec_ok, 1)
            dve.wait_ge(rec_ok, g + 1)
            if reused is not None:
                dve.wait_ge(att_out[s % 2], reused)
            v.tensor_tensor(att[s % 2][:].rearrange("p t (j d) -> p (t j) d", d=HEAD_DIM), u[:, :, 0:HEAD_DIM],
                            u_rec[:].unsqueeze(2).to_broadcast([P, REP * TT, HEAD_DIM]), ALU.mult
                            ).then_inc(att_ok, 1)

        def dve_steps(i, first=False, last=False):
            base = 4 * i
            for s in range(4):
                g = base + s
                for kt in range(TT):
                    for a in range(2):
                        nn = 8 * s + 2 * kt + a + S_AHEAD
                        if not (last and nn >= 32):
                            maxima(base, nn)
                        if kt == 2 and a == 0 and not (last and s == 3):
                            n = s + 1
                            reused = None if first and s == 0 else 32 * i + (32 if n >= 2 else 0)
                            split_shift(g + 1, n % 4, reused)
                        if kt == 3 and a == 0 and not (first and s == 0):
                            reused = None if first and s < 3 else 16 * (2 * i) + 16 * ((s - 3) // 2 + 1)
                            normalise(g - 1, (s + 3) % 4, reused)

        for nn in range(S_AHEAD):
            maxima(0, nn)
            if nn == 8:
                split_shift(0, 0, None)
        dve_steps(0, first=True)
        with dve.Fori(1, GROUPS // 4 - 1) as i:
            dve_steps(i)
        dve_steps(GROUPS // 4 - 1, last=True)
        normalise(LAST_G, 3, 16 * (GROUPS // 2 - 1))

        for p in range(2):
            dve.wait_ge(att_out[p], 16 * GROUPS // 2)
        with dve.Fori(0, BATCH) as b:
            chain.enter(b, TT * 7 + 1)
            for kt in range(KT):
                dve.wait_ge(ah_ok, 4 * b + kt + 1)
                v.tensor_tensor(al[0][:, kt, :], BANK[kt], ah[0][:, kt, :].bitcast(FP32), ALU.subtract
                                ).then_inc(al_ok, 1)
            row = [fac_row[:, a, OT:OT + 4, :].rearrange("p t c -> p (t c)") for a in range(2)]
            for t in range(TT):
                y = oy[0][:]
                dve.wait_ge(o_mm, 4 * b + t + 1)
                v.tensor_tensor(y, BANK[4 + t % 2], row[0], ALU.mult).then_inc(oy_ok, 1)
                dve.wait_ge(oy_ok, 4 * b + t + 1)
                chain.link(v.tensor_tensor(o_alt[:], y, y, ALU.is_equal))
                chain.link(v.scalar_tensor_tensor(o_alt[:], o_alt[:], GUARD, y, ALU.mult, ALU.min))
                chain.link(v.tensor_scalar(o_alt[:], o_alt[:], -GUARD, None, ALU.max))
                chain.link(v.tensor_tensor(oz[:], y, row[1], ALU.mult))
                chain.link(v.tensor_scalar(o_mask[:], oz[:], 0.0, None, ALU.is_equal))
                settle(dve)
                chain.link(v.copy_predicated(o_alt[:], o_mask[:], y))
                dve.wait_ge(x1_out, 16 * b)
                v.tensor_tensor(x1[:, t, :], x_sb[:, bass.ds(4 * b + t, 1), :].rearrange("p o c -> p (o c)"),
                                o_alt[:], ALU.add).then_inc(x1_ok, 1)
                dve.wait_ge(x1_ok, 4 * b + t + 1)
                chain.link(v.bn_stats(st2[:, t, :], x1[:, t, :]))
            settle(dve)
            for t in range(TT):
                last = v.bn_aggr(mv2[:, t, :], st2[:, t, :])
            chain.link(last)
            v.tensor_scalar(ve2[:], mv2[:, :, 1], EPS, None, ALU.add).then_inc(ve2_ok, 1)
            dve.wait_ge(rstd2_ok, b + 1)
            dve.wait_ge(x2T_mm, 4 * b)
            for t in range(TT):
                v.tensor_scalar(xn2[:, t, :], x1[:, t, :], mv2[:, t, 0:1], rstd2[:, t:t + 1],
                                ALU.subtract, ALU.mult).then_inc(xn2_ok, 1)
            chain.leave(BATCH)

        with dve.Fori(0, IT // 2) as i:
            for p in range(2):
                dve.wait_ge(d_ok[p], i + 1)
                v.tensor_reduce(dsum[:, :, bass.ds(2 * i + p, 1)], wn[p][:], AX.X, ALU.add,
                                apply_absolute_value=True).then_inc(tile_done[p], 3)
        for p in range(2):
            dve.wait_ge(tile_done[p], 3 * (IT // 2))
        v.tensor_reduce(dtot[:], dsum[:], AX.X, ALU.add).then_inc(dtot_ok, 1)
        dve.wait_ge(ctot_mm, 1)
        v.tensor_scalar(coeff[:], BANK[7][:, 0:3], 1.0 / (INTER * HID), None, ALU.mult).then_inc(coeff_ok, 1)
        dve.wait_ge(coeff_ok, 1)
        with dve.Fori(0, IT // 2) as i:
            for p in range(2):
                dve.wait_ge(sg_ok[p], i + 1)
                for k in range(3):
                    v.scalar_tensor_tensor(sg[p][:, k, :], sg[p][:, k, :], coeff[:, k:k + 1], mn[p][:, k, :],
                                           ALU.mult, ALU.add).then_inc(tile_done[p], 1)

        with dve.Fori(0, BATCH) as b:
            for kt in range(KT):
                dve.wait_ge(fxh_ok, 4 * b + kt + 1)
                v.tensor_tensor(fxl[:, kt, :], x2T[:, bass.ds(4 * b + kt, 1), :].rearrange("p o c -> p (o c)"),
                                fxh[:, kt, :].bitcast(FP32), ALU.subtract).then_inc(fxl_ok, 1)
            with dve.Fori(0, IT // 2) as i:
                for p in range(2):
                    use = (IT // 2) * b + i
                    for k, src in enumerate((w1T, w3T, w2T)):
                        if k < 2:
                            dve.wait_ge(wh_a[p], 2 * use + k + 1)
                        else:
                            dve.wait_ge(wh_p[p], use + 1)
                        v.tensor_tensor(wl[p][:, k, :], src[:, bass.ds(2 * i + p, 1), :].rearrange("p o c -> p (o c)"),
                                        wh[p][:, k, :].bitcast(FP32), ALU.subtract).then_inc(wl_ok[p], 1)
                    dve.wait_ge(silu_ok[p], use + 1)
                    dve.wait_ge(u_mm[p], use + 1)
                    dve.wait_ge(hh_ok[p], use)
                    v.tensor_tensor(hid[p][:], gate[p][:], BANK[2 + p], ALU.mult).then_inc(h_ok[p], 1)
                    dve.wait_ge(hh_ok[p], use + 1)
                    v.tensor_tensor(hl[p][:], hid[p][:], hh[p][:].bitcast(FP32), ALU.subtract).then_inc(hl_ok[p], 1)
            for t in range(TT):
                dve.wait_ge(d_mm[1], (IT // 2) * (b + 1))
                dve.wait_ge(x1r_in, 16 * (b + 1))
                dve.wait_ge(out_done[t % 2], 16 * (2 * b + t // 2))
                v.tensor_tensor(ob[t % 2][:], BANK[4 + t], x1r[:, t, :], ALU.add).then_inc(ob_ok, 1)

    @block.tensor
    def _(pe):
        mm, tr = nc.tensor.matmul, nc.tensor.transpose
        pe.wait_ge(const_ok, 5)
        for m in range(WTILES):
            pe.wait_ge(sgn_ok, m + 1)
            positive(pe, signs_ok, m - 3)
            for kt in range(KT):
                last = tr(BANK[m % 4].bitcast(BF16)[:, kt * P:(kt + 1) * P], w_sgn[:, m, kt * P:(kt + 1) * P], ident16[:])
            last.then_inc(sgnT_ok, 1)
        pe.wait_ge(signs_ok, WTILES)

        with pe.Fori(0, 2) as i:
            for p in range(2):
                pe.wait_ge(xn_ok[p], 4 * (i + 1))
                pe.wait_ge(xl_ok[1 - p], 4 * (i + p))
                for kt in range(KT):
                    for t in range(TT):
                        last = tr(BANK[kt][:, t * P:(t + 1) * P], xn[p][:, t, kt * P:(kt + 1) * P], ident[:])
                    last.then_inc(xT_ok[p], 1)
            for p in range(2):
                b = 2 * i + p
                pe.wait_ge(xl_ok[p], 4 * (i + 1))
                for m in range(5):
                    pe.wait_ge(yq_ok, 5 * b + max(m - 2, 0))
                    w = slice(m * P, (m + 1) * P)
                    for kt in range(KT):
                        mm(BANK[4 + m % 3], signs[:, kt, w], xh[p][:, kt, :], start=(kt == 0), stop=False)
                        last = mm(BANK[4 + m % 3], signs[:, kt, w], xl[p][:, kt, :], start=False, stop=(kt == KT - 1))
                    last.then_inc(q_mm, 1)
                pe.wait_ge(vy_ok, b)
                w = slice(VTILE * P, (VTILE + 1) * P)
                for t in range(TT):
                    o = BANK[7][:, t * P:(t + 1) * P]
                    for kt in range(KT):
                        mm(o, xh[p][:, kt, t * P:(t + 1) * P], signs[:, kt, w], start=(kt == 0), stop=False)
                        last = mm(o, xl[p][:, kt, t * P:(t + 1) * P], signs[:, kt, w], start=False, stop=(kt == KT - 1))
                last.then_inc(v_mm[p], 1)

        pe.wait_ge(v_ok, BATCH)
        pe.wait_ge(slot_init, 14)

        def scores(i, nn):
            rel, j, half_tile = nn // 8, nn % 8 // 2, nn % 2
            s = rel % 4
            if nn % 8 == 0:
                pe.wait_ge(slot_in[s], 48 * (i + rel // 4 + 1))
                positive(pe, cleared, 4 * i + rel - 3)
            positive(pe, s_max, 32 * i + nn - 1)
            for a in range(2):
                q = 2 * half_tile + a
                last = mm(BANK[q], q_slot[s][:, j, q * P:(q + 1) * P], k_slot[s][:], start=True, stop=True)
            last.then_inc(s_mm, 1)

        def transpose_maxima(g, s, before):
            pe.wait_ge(s_max, 8 * g + 8)
            positive(pe, att_ok, before)
            tr(BANK[7][0:REP * TT, 0:P], nmx[s % 2][:], ident[:]).then_inc(mT_ok, 1)

        def shifted_scores(i, s, kt, j):
            g = 4 * i + s
            if kt == 0 and j == 0:
                pe.wait_ge(shift_in[s], 32 * (i + 1))
            positive(pe, exp_ok, 16 * g + 4 * kt + j - 1)
            mm(BANK[4 + j % 2], k_slot[s][:, kt * P:(kt + 1) * P], q_slot[s][:, j, :],
               start=True, stop=True).then_inc(t_mm, 1)

        def weigh_values(g, s, kt):
            pe.wait_ge(exp_ok, 16 * g + 4 * kt + 4)
            if kt == 0:
                pe.wait_ge(vs_ok, g + 1)
                positive(pe, u_ok, g)
            for j in range(REP):
                last = mm(psum[32 * j:32 * j + 32, 6, :], v_slot[s % 2][:, kt, :], probs[kt % 2][:, j, :],
                          start=(kt == 0), stop=(kt == TT - 1))
            last.then_inc(pv_mm, 1)

        def transpose_values(g, lows):
            pe.wait_ge(u_ok, g + 1)
            pe.wait_ge(sh_lo, lows)
            for t in range(TT):
                last = tr(BANK[7][:, t * P:(t + 1) * P], u_sb[:, t * P:(t + 1) * P], ident[:])
            last.then_inc(uT_ok, 1)

        def pe_steps(i, first=False, last=False):
            for s in range(4):
                g = 4 * i + s
                for kt in range(TT):
                    for j in range(REP):
                        shifted_scores(i, s, kt, j)
                        nn = 8 * s + 2 * kt + j // 2 + S_AHEAD
                        if j % 2 == 1 and not (last and nn >= 32):
                            scores(i, nn)
                    if kt > 0:
                        weigh_values(g, s, kt - 1)
                    elif not (first and s == 0):
                        weigh_values(g - 1, s + 3, TT - 1)
                    if kt == 1 and not (last and s == 3):
                        transpose_maxima(g + 1, s + 1, g - 1)
                    if kt == 2 and last and s == 3:
                        pe.wait_ge(att_ok, g - 1)
                    if kt == 2 and not (first and s == 0):
                        transpose_values(g - 1, g + 1 if last and s == 3 else g + 2)

        for nn in range(S_AHEAD):
            scores(0, nn)
            if nn == 8:
                transpose_maxima(0, 0, 0)
        pe_steps(0, first=True)
        with pe.Fori(1, GROUPS // 4 - 1) as i:
            pe_steps(i)
        pe_steps(GROUPS // 4 - 1, last=True)
        weigh_values(LAST_G, 3, TT - 1)
        pe.wait_ge(att_ok, LAST_G)
        transpose_values(LAST_G, GROUPS)

        with pe.Fori(0, BATCH) as b:
            pe.wait_ge(an_in, 32 * (b + 1))
            pe.wait_ge(x2T_ok, 4 * b)
            pe.wait_ge(att_ok, GROUPS)
            for kt in range(KT):
                for t in range(TT):
                    last = tr(BANK[kt][:, t * P:(t + 1) * P], an[0][:, t, kt * P:(kt + 1) * P], ident[:])
                last.then_inc(aT_ok, 1)
            pe.wait_ge(al_ok, 4 * (b + 1))
            for t in range(TT):
                pe.wait_ge(oy_ok, 4 * b + max(t - 1, 0))
                for kt in range(KT):
                    mm(BANK[4 + t % 2], ah[0][:, kt, t * P:(t + 1) * P], signs_o[:, kt, :], start=(kt == 0), stop=False)
                    last = mm(BANK[4 + t % 2], al[0][:, kt, t * P:(t + 1) * P], signs_o[:, kt, :],
                              start=False, stop=(kt == KT - 1))
                last.then_inc(o_mm, 1)
            pe.wait_ge(xn2_ok, 4 * (b + 1))
            for kt in range(KT):
                for t in range(TT):
                    last = tr(BANK[kt][:, t * P:(t + 1) * P], xn2[:, t, kt * P:(kt + 1) * P], ident[:])
                last.then_inc(x2T_mm, 1)
        pe.wait_ge(dtot_ok, 1)
        mm(BANK[7][:, 0:3], ones[:], dtot[:], start=True, stop=True).then_inc(ctot_mm, 1)
        pe.wait_ge(x2T_ok, NT)
        with pe.Fori(0, IT // 2) as i:
            for p in range(2):
                pe.wait_ge(wT_ok[p], 3 * i)
                for k in range(3):
                    pe.wait_ge(tile_done[p], 3 * (IT // 2) + 3 * i + k + 1)
                    for t in range(TT):
                        last = tr(BANK[3 * p + k][:, t * P:(t + 1) * P], sg[p][:, k, t * P:(t + 1) * P], ident[:])
                    last.then_inc(wT_mm[p], 1)
        for p in range(2):
            pe.wait_ge(wT_ok[p], 3 * (IT // 2))
        pe.wait_ge(coeff_ok, 1)

        def three(o, lhs_hi, lhs_lo, rhs_hi, rhs_lo, first, final):
            mm(o, lhs_hi, rhs_hi, start=first, stop=False)
            mm(o, lhs_hi, rhs_lo, start=False, stop=False)
            return mm(o, lhs_lo, rhs_hi, start=False, stop=final)

        def gate_up(p, use):
            for k, (b0, ok, done) in enumerate(((0, silu_ok, g_mm), (2, h_ok, u_mm))):
                pe.wait_ge(wl_ok[p], 3 * use + k + 1)
                pe.wait_ge(ok[p], use)
                for kt in range(KT):
                    c = slice(kt * P, (kt + 1) * P)
                    last = three(BANK[b0 + p], wh[p][:, k, c], wl[p][:, k, c], fxh[:, kt, :], fxl[:, kt, :],
                                 kt == 0, kt == KT - 1)
                last.then_inc(done[p], 1)

        def down(p, use, first, final):
            pe.wait_ge(wl_ok[p], 3 * use + 3)
            pe.wait_ge(hl_ok[p], use + 1)
            for t in range(TT):
                c = slice(t * P, (t + 1) * P)
                last = three(BANK[4 + t], hh[p][:, c], hl[p][:, c], wh[p][:, 2, :], wl[p][:, 2, :], first, final)
            last.then_inc(d_mm[p], 1)

        with pe.Fori(0, BATCH) as b:
            pe.wait_ge(fxl_ok, 4 * (b + 1))
            gate_up(0, (IT // 2) * b)
            gate_up(1, (IT // 2) * b)
            pe.wait_ge(ob_ok, 4 * b)
            down(0, (IT // 2) * b, True, False)
            with pe.Fori(1, IT // 2) as i:
                use = (IT // 2) * b + i
                gate_up(0, use)
                down(1, use - 1, False, False)
                gate_up(1, use)
                down(0, use, False, False)
            down(1, (IT // 2) * (b + 1) - 1, False, True)

    ctx.close()


_INS = ["L0_attn_hidden_states", "L0_attn_q_weight", "L0_attn_q_scale", "L0_attn_k_weight", "L0_attn_k_scale",
        "L0_attn_v_weight", "L0_attn_v_scale", "L0_attn_o_weight", "L0_attn_o_scale",
        "L0_ffn_w1", "L0_ffn_mean_w1", "L0_ffn_w2", "L0_ffn_mean_w2", "L0_ffn_w3", "L0_ffn_mean_w3"]
_OUTS = [((BATCH, SEQ, HID), "float32")]


def kernel(**inputs):
    import numpy as _np
    import concourse.bacc as _bacc
    from concourse import mybir as _mybir
    from concourse.bass_utils import run_bass_kernel_spmd as _run

    nc = _bacc.Bacc("TRN2", target_bir_lowering=False, num_devices=1)
    arrays, args = {}, []
    for name in _INS:
        a = _np.ascontiguousarray(inputs[name])
        arrays[f"in_{name}_dram"] = a
        args.append(nc.dram_tensor(f"in_{name}_dram", a.shape, _mybir.dt.from_np(a.dtype), kind="ExternalInput").ap())
    for i, (shape, dtype) in enumerate(_OUTS):
        dt = _mybir.dt.from_np(_np.dtype(dtype))
        args.append(nc.dram_tensor(f"out_{i}_dram", shape, dt, kind="ExternalOutput").ap())
    decoder_layer(nc, *args)
    r = _run(nc, [arrays], core_ids=[0])
    return r.results[0]["out_0_dram"]
```

```python
import numpy as np
import concourse.bass as bass
from concourse import mybir
from contextlib import ExitStack

FP32 = mybir.dt.float32
FP32R = mybir.dt.float32r
BF16 = mybir.dt.bfloat16
I32 = mybir.dt.int32
ALU = mybir.AluOpType
ACT = mybir.ActivationFunctionType
AX = mybir.AxisListType

P = 128
BATCH, SEQ, HID = 4, 512, 512
HEADS, KV_HEADS = 32, 8
HEAD_DIM = HID // HEADS
REP = HEADS // KV_HEADS
GROUPS = BATCH * KV_HEADS
INTER = 1792
KT = HID // P
TT = SEQ // P
NT = BATCH * TT
IT = INTER // P
QT, KTILE, VTILE, OT = 0, 4, 5, 6
WTILES = 10
BIT_IN = 768
EPS = 1e-5
FLT_MAX = float(np.finfo(np.float32).max)
GUARD = 1e6
SHIFT_MAX = 3e38
STACK = 96
SHIFT_ROW = 64


def positive(eng, sem, value):
    if not isinstance(value, int) or value > 0:
        eng.wait_ge(sem, value)


def settle(eng):
    eng.nop(nofuse=True)


RING = 4


class Chain:

    def __init__(self, eng, sem):
        self.eng, self.sem, self.base, self.k, self.saved = eng, sem, 0, 0, 0

    def link(self, ins):
        ins.then_inc(self.sem, 1)
        self.k += 1
        self.eng.wait_ge(self.sem, self.base + self.k)

    def enter(self, i, per):
        self.saved, self.per = self.base + self.k, per
        self.base, self.k = self.saved + i * per, 0

    def leave(self, times):
        assert self.k == self.per, (self.k, self.per)
        self.base, self.k = self.saved + times * self.per, 0


def decoder_layer(nc, x, q_w, q_s, k_w, k_s, v_w, v_s, o_w, o_s, w1, m1, w2, m2, w3, m3, out):
    ctx = ExitStack()

    def sem(name):
        return ctx.enter_context(nc.semaphore(name))

    def sems(name, n):
        return [sem(f"{name}{i}") for i in range(n)]

    def region(scope):
        return lambda name, shape, dt=FP32: scope.enter_context(nc.sbuf_tensor(name, shape, dt))

    q_dram = nc.dram_tensor("q_parts", [GROUPS, 2, HEAD_DIM, REP, SEQ], FP32, kind="Internal").ap()
    k_dram = nc.dram_tensor("k_stack", [GROUPS, 4 * HEAD_DIM, SEQ], FP32, kind="Internal").ap()
    fac_dram = nc.dram_tensor("factors", [2, WTILES, P], FP32, kind="Internal").ap()
    att_dram = nc.dram_tensor("attended", [GROUPS // 4, TT, P, 4 * 64], FP32, kind="Internal").ap()
    x1_dram = nc.dram_tensor("residual", [NT, P, HID], FP32, kind="Internal").ap()

    keep = region(ctx)
    ident = keep("ident", [P, P])
    ident16 = keep("ident16", [P, P], BF16)
    half = keep("minus_half", [P, NT])
    ones = keep("ones", [P, P])
    signs_o = keep("signs_o", [P, KT, HID], FP32R)
    fac_row = keep("fac_row", [P, 2, WTILES - VTILE, P])
    dsum = keep("dsum", [P, 3, IT])
    dtot = keep("dtot", [P, 3])
    coeff = keep("coeff", [P, 3])
    until_c = ExitStack()
    mid = region(until_c)
    v_sb = mid("v_sb", [P, GROUPS, TT, HEAD_DIM])

    with ExitStack() as scope:
        sb = region(scope)
        x_sb = sb("x_sb", [P, NT, HID])
        w_nat = sb("w_nat", [P, WTILES, HID])
        w_sgn = sb("w_sgn", [P, WTILES, HID], BF16)
        signs = sb("signs_qkv", [P, KT, BIT_IN], FP32R)
        scl = sb("scl", [P, WTILES])
        wstat = sb("wstat", [P, 6, WTILES])
        stats = sb("stats", [P, NT, 6])
        mv = sb("mv", [P, NT, 2])
        ve = sb("ve", [P, NT])
        rstd = sb("rstd", [P, NT])
        xn = [sb(f"xn{p}", [P, TT, HID]) for p in range(2)]
        xh = [sb(f"xh{p}", [P, KT, SEQ], FP32R) for p in range(2)]
        xl = [sb(f"xl{p}", [P, KT, SEQ], FP32R) for p in range(2)]
        yq = [w_nat[:, 5 * p:5 * p + 5, :] for p in range(2)]
        q_hi = sb("q_hi", [P, 5, SEQ], FP32R)
        q_lo = sb("q_lo", [P, 5, SEQ], FP32R)
        g_mask = sb("g_mask", [P, SEQ], I32)
        g_alt = sb("g_alt", [P, SEQ])
        vy = sb("vy", [P, TT, P])
    with ExitStack() as scope:
        sb = region(scope)
        q_slot = [sb(f"q_slot{s}", [STACK, REP, SEQ], FP32R) for s in range(4)]
        k_slot = [sb(f"k_slot{s}", [STACK, SEQ], FP32R) for s in range(4)]
        v_slot = [sb(f"v_slot{s}", [P, TT, 32]) for s in range(2)]
        probs = [sb(f"probs{s}", [P, REP, SEQ]) for s in range(2)]
        nmx = [sb(f"nmx{s}", [P, REP * TT]) for s in range(2)]
        shift = [sb(f"shift{s}", [REP * TT, 2, P], FP32R) for s in range(2)]
        u_sb = sb("u_sb", [P, SEQ])
        u_rec = sb("u_rec", [P, REP * TT])
        att = [sb(f"att{s}", [P, TT, 64]) for s in range(2)]
        fw = [sb(f"fw{s}", [P, 3, HID]) for s in range(2)]
        fm = [sb(f"fm{s}", [P, 3, HID]) for s in range(2)]
    until_c.close()
    late = region(ctx)
    w1T = late("w1T", [P, IT, HID])
    w3T = late("w3T", [P, IT, HID])
    w2T = late("w2T", [P, IT, HID])
    fxh = late("fxh", [P, KT, SEQ], FP32R)
    fxl = late("fxl", [P, KT, SEQ], FP32R)
    an = late("an", [P, TT, HID])
    ah = late("ah", [P, KT, SEQ], FP32R)
    al = late("al", [P, KT, SEQ], FP32R)
    x1 = late("x1", [P, TT, HID])
    oy = late("oy", [P, SEQ])
    o_mask = late("o_mask", [P, SEQ], I32)
    o_alt = late("o_alt", [P, SEQ])
    st2 = late("st2", [P, TT, 6])
    mv2 = late("mv2", [P, TT, 2])
    ve2 = late("ve2", [P, TT])
    rstd2 = late("rstd2", [P, TT])
    with ExitStack() as scope:
        sb = region(scope)
        wn = [sb(f"wn{p}", [P, 3, HID]) for p in range(RING)]
        mn = [sb(f"mn{p}", [P, 3, HID]) for p in range(RING)]
    with ExitStack() as scope:
        sb = region(scope)
        wh = [sb(f"wh{p}", [P, 2, HID], FP32R) for p in range(2)]
        wl = [sb(f"wl{p}", [P, 2, HID], FP32R) for p in range(2)]
        dh = [sb(f"dh{p}", [P, HID], FP32R) for p in range(2)]
        dl = [sb(f"dl{p}", [P, HID], FP32R) for p in range(2)]
        gate = sb("gate", [P, SEQ])
        hh = [sb(f"hh{p}", [P, SEQ], FP32R) for p in range(2)]
        hl = [sb(f"hl{p}", [P, SEQ], FP32R) for p in range(2)]
        res = sb("res", [P, TT, HID])

    psum = ctx.enter_context(nc.psum_tensor("psum", [P, 8, 512], FP32))
    BANK = [psum[:, i, :] for i in range(8)]

    x_in = sems("x_in", BATCH)
    w_in = sems("w_in", 3)
    scl_in = sem("scl_in")
    const_ok = sem("const_ok")
    wstat_ok = sem("wstat_ok")
    sgn_ok = sem("sgn_ok")
    sgnT_ok = sem("sgnT_ok")
    signs_ok = sem("signs_ok")
    fac_out = sem("fac_out")
    fac_in = sem("fac_in")
    stat_ch = sem("stat_ch")
    rstd_ok = sem("rstd_ok")
    dve_ch = sem("dve_ch")
    xn_ok = sems("xn_ok", 2)
    xT_ok = sems("xT_ok", 2)
    xh_ok = sems("xh_ok", 2)
    xl_ok = sems("xl_ok", 2)
    q_mm = sem("q_mm")
    yq_ok = sem("yq_ok")
    yg_ok = sem("yg_ok")
    qh_ok = sem("qh_ok")
    ql_ok = sem("ql_ok")
    part_out = sems("part_out", 5)
    v_mm = sems("v_mm", 2)
    vy_ok = sem("vy_ok")
    v_ok = sem("v_ok")

    slot_in = sems("slot_in", 4)
    cleared = sem("cleared")
    slot_init = sem("slot_init")
    vs_ok = sem("vs_ok")
    s_mm = sem("s_mm")
    s_max = sem("s_max")
    mT_ok = sem("mT_ok")
    sh_hi = sem("sh_hi")
    sh_lo = sem("sh_lo")
    shift_in = sems("shift_in", 4)
    t_mm = sem("t_mm")
    exp_ok = sem("exp_ok")
    pv_mm = sem("pv_mm")
    u_ok = sem("u_ok")
    uT_ok = sem("uT_ok")
    rec_ok = sem("rec_ok")
    att_ok = sem("att_ok")
    att_out = sems("att_out", 2)

    fw_in = sems("fw_in", 2)
    fd_ok = sem("fd_ok")
    fsum_ok = sem("fsum_ok")

    an_in = sem("an_in")
    x_again = sem("x_again")
    aT_ok = sem("aT_ok")
    ah_ok = sem("ah_ok")
    al_ok = sem("al_ok")
    o_mm = sem("o_mm")
    oy_ok = sem("oy_ok")
    x1_ok = sem("x1_ok")
    x1_out = sem("x1_out")
    c_ch = sem("c_ch")
    ve2_ok = sem("ve2_ok")
    rstd2_ok = sem("rstd2_ok")
    xn2_ok = sem("xn2_ok")
    x2T_mm = sem("x2T_mm")
    fxh_ok = sem("fxh_ok")
    fxl_ok = sem("fxl_ok")
    dtot_ok = sem("dtot_ok")
    ctot_mm = sem("ctot_mm")
    coeff_ok = sem("coeff_ok")
    wn_in = sems("wn_in", RING)
    d_ok = sem("d_ok")
    sg_ok = sem("sg_ok")
    w_ok = sem("w_ok")
    wT_mm = sem("wT_mm")
    wT_ok = sem("wT_ok")
    wh_ok = sem("wh_ok")
    wl_ok = sem("wl_ok")
    dh_ok = sem("dh_ok")
    dl_ok = sem("dl_ok")
    g_mm = sem("g_mm")
    u_mm = sem("u_mm")
    silu_ok = sem("silu_ok")
    h_ok = sem("h_ok")
    hh_ok = sem("hh_ok")
    hl_ok = sem("hl_ok")
    d_mm = sem("d_mm")
    res_in = sem("res_in")
    res_ok = sem("res_ok")
    out_done = sem("out_done")

    LAST_G = GROUPS - 1
    GATE, UP, DOWN = 0, 1, 2
    NORM_BANK = (6, 7, GATE, UP)
    NORM_STEP = KT + TT
    LAG = 3
    CREDIT = 2
    S_AHEAD = 14
    S_USES = GROUPS * 8

    block = ctx.enter_context(nc.Block())

    @block.sync
    def _(sp):
        for b in range(BATCH):
            sp.dma_start(x_sb[:, b * TT:(b + 1) * TT, :],
                         x[b].rearrange("(t p) c -> p t c", p=P)).then_inc(x_in[b], 16)
        sp.wait_ge(wstat_ok, 3)
        sp.dma_start(fac_dram.rearrange("a w p -> p a w"), wstat[:, 3:5, :],
                     allow_slow_non_contiguous=True).then_inc(fac_out, 16)
        sp.wait_ge(fac_out, 16)
        for a in range(2):
            sp.dma_start(fac_row[:, a].rearrange("p w c -> p (w c)"),
                         fac_dram[a, VTILE:].rearrange("w p -> (w p)").unsqueeze(0).to_broadcast([P, (WTILES - VTILE) * P])
                         ).then_inc(fac_in, 16)

        with sp.Fori(0, 2) as i:
            for p in range(2):
                b = 2 * i + p
                for m in range(5):
                    for part, (src, ready) in enumerate(((q_hi, qh_ok), (q_lo, ql_ok))):
                        sp.wait_ge(ready, 5 * b + m + 1)
                        if m < 4:
                            for half_tile in range(2):
                                g = 8 * b + 2 * m + half_tile
                                dst = q_dram[bass.ds(g, 1), part].rearrange("o d j t -> (o j) d t")
                                rows = src[64 * half_tile:64 * half_tile + 64, m, :].bitcast(FP32)
                                sp.dma_start(dst, rows).then_inc(part_out[m], 16)
                        else:
                            for copy in range(2):
                                r = (2 * part + copy) * HEAD_DIM
                                dst = k_dram[bass.ds(8 * b, 8), r:r + HEAD_DIM, :]
                                sp.dma_start(dst, src[:, m, :].bitcast(FP32)).then_inc(part_out[m], 16)

        for m in range(5):
            sp.wait_ge(part_out[m], BATCH * 64)
        sp.wait_ge(v_ok, BATCH)
        sp.wait_ge(slot_init, 14)

        def load_group(g, s):
            for copy in range(2):
                sp.dma_start(q_slot[s][32 * copy:32 * copy + 32].bitcast(FP32),
                             q_dram[bass.ds(g, 1)].rearrange("o l d j t -> (o l d) j t")
                             ).then_inc(slot_in[s], 16)
            sp.dma_start(k_slot[s][0:SHIFT_ROW].bitcast(FP32),
                         k_dram[bass.ds(g, 1)].rearrange("o r t -> (o r) t")).then_inc(slot_in[s], 16)

        def load_shift(g, s):
            for part, ready in enumerate((sh_hi, sh_lo)):
                sp.wait_ge(ready, g + 1)
                sp.dma_start(q_slot[s][SHIFT_ROW + part:SHIFT_ROW + part + 1].bitcast(FP32).rearrange("o j (t c) -> o (j t) c", c=P),
                             shift[s % 2][:, part, :].bitcast(FP32)).then_inc(shift_in[s], 16)

        def store_att(i, s):
            sp.wait_ge(att_ok, 4 * i + s + 1)
            sp.dma_start(att_dram[bass.ds(i, 1), :, :, 64 * s:64 * s + 64].rearrange("o t p c -> (o p) t c"),
                         att[s % 2][:]).then_inc(att_out[s % 2], 16)

        for g in range(3):
            load_group(g, g)
        load_shift(0, 0)

        def load_tile(e, w_dst, m_dst, done):
            for k, (w, m) in enumerate(((w1, m1), (w3, m3))):
                sp.dma_start(w_dst[:, k, :], w[bass.ds(e * P, P), :]).then_inc(done, 16)
                sp.dma_start(m_dst[:, k, :], m[bass.ds(e * P, P), :]).then_inc(done, 16)
            for w, dst in ((w2, w_dst), (m2, m_dst)):
                sp.dma_start(dst[:, 2, :].rearrange("p (t c) -> p t c", c=P),
                             w[:, bass.ds(e * P, P)].rearrange("(t p) c -> p t c", p=P)).then_inc(done, 16)

        def sp_steps(i, first=False, last=False):
            for s in range(4):
                g = 4 * i + s
                if s % 2 == 0 and not last:
                    if not first:
                        sp.wait_ge(fsum_ok, 2 * i + s // 2 - 1)
                        settle(sp)
                    load_tile(2 * i + s // 2, fw[s // 2], fm[s // 2], fw_in[s // 2])
                if not (last and s > 0):
                    positive(sp, t_mm, 16 * g)
                    load_group(g + 3, (s + 3) % 4)
                if not (last and s == 3):
                    load_shift(g + 1, (s + 1) % 4)
                if not (first and s == 0):
                    store_att(*((i, s - 1) if s else (i - 1, 3)))

        sp_steps(0, first=True)
        with sp.Fori(1, GROUPS // 4 - 1) as i:
            sp_steps(i)
        sp_steps(GROUPS // 4 - 1, last=True)
        store_att(GROUPS // 4 - 1, 3)
        for s in range(2):
            sp.wait_ge(att_out[s], 16 * GROUPS // 2)

        def load_batch(b):
            settle(sp)
            for part in range(2):
                sp.dma_start(an[:, :, 256 * part:256 * part + 256],
                             att_dram[bass.ds(2 * b + part, 1)].rearrange("o t p c -> (o p) t c")).then_inc(an_in, 16)
            sp.dma_start(x1[:], x[bass.ds(b, 1)].rearrange("o (t p) c -> (o p) t c", p=P)).then_inc(x_again, 16)

        def store_residual(b):
            sp.wait_ge(x1_ok, 4 * (b + 1))
            settle(sp)
            sp.dma_start(x1_dram[bass.ds(4 * b, 4)].rearrange("t p c -> p t c"), x1[:]).then_inc(x1_out, 16)

        sp.wait_ge(fsum_ok, IT)
        load_batch(0)
        for e in range(IT):
            if e >= RING:
                sp.wait_ge(wT_mm, 3 * (e - RING + 1))
            load_tile(e, wn[e % RING], mn[e % RING], wn_in[e % RING])
            if e == IT - RING:
                store_residual(0)

        def finish_batch(b):
            settle(sp)
            sp.wait_ge(x1_out, 16 * (b + 1))
            settle(sp)
            sp.dma_start(res[:], x1_dram[bass.ds(4 * b, TT)].rearrange("t p c -> p t c")).then_inc(res_in, 16)
            for t in range(TT):
                sp.wait_ge(res_ok, CREDIT + 4 * b + t + 1)
                settle(sp)
                sp.dma_start(out[bass.ds(b, 1), t * P:(t + 1) * P, :].rearrange("o p c -> (o p) c"),
                             res[:, t, :]).then_inc(out_done, 16)

        sp.wait_ge(wT_mm, 3 * IT)
        with sp.Fori(0, BATCH - 1) as b:
            sp.wait_ge(x2T_mm, 4 * (b + 1))
            settle(sp)
            sp.wait_ge(x1_out, 16 * (b + 1))
            settle(sp)
            sp.wait_ge(xn2_ok, 4 * (b + 1))
            load_batch(b + 1)
            store_residual(b + 1)
            finish_batch(b)
            sp.wait_ge(out_done, 64 * (b + 1))
            settle(sp)
        finish_batch(BATCH - 1)
        sp.wait_ge(out_done, 64 * BATCH)


    @block.gpsimd
    def _(pool):
        nc.gpsimd.memset(ident[:], 0.0).then_inc(const_ok, 1)
        pool.wait_ge(const_ok, 1)
        nc.gpsimd.affine_select(out=ident[:], in_=ident[:], compare_op=ALU.not_equal, fill=1.0, base=0,
                                pattern=[[-1, P]], channel_multiplier=1).then_inc(const_ok, 1)
        pool.wait_ge(const_ok, 2)
        nc.gpsimd.tensor_copy(ident16[:], ident[:]).then_inc(const_ok, 1)
        nc.gpsimd.memset(half[:], -0.5).then_inc(const_ok, 1)
        nc.gpsimd.memset(ones[:], 1.0).then_inc(const_ok, 1)
        pool.wait_ge(const_ok, 5)
        pool.wait_ge(stat_ch, 2 * NT + 1)
        nc.gpsimd.tensor_tensor(rstd[:], ve[:], half[:], ALU.pow).then_inc(rstd_ok, 1)

        with pool.Fori(0, 2) as i:
            for p in range(2):
                b = 2 * i + p
                for m in range(5):
                    pool.wait_ge(yg_ok, 5 * b + m + 1)
                    pool.wait_ge(part_out[m], 64 * b)
                    settle(pool)
                    nc.gpsimd.tensor_copy(q_hi[:, m, :], g_alt[:]).then_inc(qh_ok, 1)

        pool.wait_ge(v_ok, BATCH)
        for m in range(5):
            pool.wait_ge(part_out[m], BATCH * 64)
        for s in range(4):
            nc.gpsimd.memset(q_slot[s][SHIFT_ROW:STACK].bitcast(FP32), 0.0).then_inc(slot_init, 1)

        def clear_shift(g, s):
            settle(pool)
            nc.gpsimd.memset(q_slot[s][SHIFT_ROW:SHIFT_ROW + 2].bitcast(FP32), 0.0).then_inc(cleared, 1)

        def fill_values(g, s):
            settle(pool)
            nc.gpsimd.tensor_copy(v_slot[s][:, :, 0:HEAD_DIM],
                                  v_sb[:, bass.ds(g, 1), :, :].rearrange("p o t d -> p (o t) d")).then_inc(vs_ok, 1)

        pool.wait_ge(slot_init, 14)
        fill_values(0, 0)
        fill_values(1, 1)

        def pool_steps(i, first=False, last=False):
            for s in range(4):
                g = 4 * i + s
                if s % 2 == 1 and not last:
                    h = s // 2
                    pool.wait_ge(vs_ok, g + 1)
                    settle(pool)
                    pool.wait_ge(fw_in[h], 96 * (i + 1))
                    nc.gpsimd.tensor_tensor(fw[h][:], fw[h][:], fm[h][:], ALU.subtract).then_inc(fd_ok, 1)
                    pool.wait_ge(fd_ok, 2 * i + h + 1)
                if not (first and s == 0):
                    if not (last and s > 0):
                        pool.wait_ge(t_mm, 16 * g)
                        pool.wait_ge(vs_ok, g + 1)
                        clear_shift(g + 3, (s + 3) % 4)
                    if not (last and s == 3):
                        pool.wait_ge(pv_mm, 4 * g)
                        if not (last and s > 0):
                            pool.wait_ge(cleared, g)
                        fill_values(g + 1, (s + 1) % 2)

        pool_steps(0, first=True)
        with pool.Fori(1, GROUPS // 4 - 1) as i:
            pool_steps(i)
        pool_steps(GROUPS // 4 - 1, last=True)

        def norm_factor(b):
            pool.wait_ge(ve2_ok, b + 1)
            nc.gpsimd.tensor_tensor(rstd2[:], ve2[:], half[:, 0:TT], ALU.pow).then_inc(rstd2_ok, 1)

        for e in range(IT):
            pool.wait_ge(wn_in[e % RING], 96 * (e // RING + 1))
            nc.gpsimd.tensor_tensor(wn[e % RING][:], wn[e % RING][:], mn[e % RING][:], ALU.subtract).then_inc(d_ok, 1)
            if e == NORM_STEP:
                norm_factor(0)
        def split_down(b, e, src, parity):
            n = IT * b + e
            pool.wait_ge(d_mm, CREDIT + n - 1)
            settle(pool)
            nc.gpsimd.tensor_copy(dh[parity][:], w2T[:, bass.ds(src, 1), :].rearrange("p o c -> p (o c)")
                                  ).then_inc(dh_ok, 1)

        pool.wait_ge(wT_ok, 3 * IT)
        with pool.Fori(0, BATCH - 1) as b:
            for e in range(LAG + NORM_STEP + 1):
                split_down(b, e, e, e % 2)
            norm_factor(b + 1)
            for e in range(LAG + NORM_STEP + 1, IT):
                split_down(b, e, e, e % 2)
        with pool.Fori(0, IT // 2) as i:
            for p in range(2):
                split_down(BATCH - 1, 2 * i + p, 2 * i + p, p)

    @block.scalar
    def _(act):
        act.nop(nofuse=True).then_inc(silu_ok, CREDIT)
        for n, (src, t0, tiles) in enumerate(((q_w, QT, 4), (k_w, KTILE, 1), (v_w, VTILE, 1), (o_w, OT, 4))):
            act.dma_start(w_nat[:, t0:t0 + tiles, :], src.rearrange("(t p) c -> p t c", p=P)
                          ).then_inc(w_in[(0, 1, 1, 2)[n]], 16)
        for src, t0, tiles in ((q_s, QT, 4), (k_s, KTILE, 1), (v_s, VTILE, 1), (o_s, OT, 4)):
            act.dma_start(scl[:, t0:t0 + tiles], src.rearrange("(t p) -> p t", p=P),
                          allow_slow_non_contiguous=True).then_inc(scl_in, 16)
        act.wait_ge(wstat_ok, 1)
        for m in range(WTILES):
            nc.scalar.activation(w_sgn[:, m, :], w_nat[:, m, :], ACT.Sign,
                                 scale=wstat[:, 2, m:m + 1]).then_inc(sgn_ok, 1)
        act.wait_ge(wstat_ok, 3)

        with act.Fori(0, 2) as i:
            for p in range(2):
                b = 2 * i + p
                for kt in range(KT):
                    act.wait_ge(xT_ok[p], 4 * i + kt + 1)
                    if kt == 0:
                        act.wait_ge(v_mm[p], i)
                    nc.scalar.activation(xh[p][:, kt, :], BANK[kt], ACT.Copy).then_inc(xh_ok[p], 1)
            for p in range(2):
                b = 2 * i + p
                for m in range(5):
                    act.wait_ge(q_mm, 5 * b + m + 1)
                    if m == 0:
                        act.wait_ge(ql_ok, 5 * (2 * i))
                    nc.scalar.activation(yq[p][:, m, :], BANK[4 + m % 3], ACT.Copy,
                                         scale=wstat[:, 3, m:m + 1]).then_inc(yq_ok, 1)

        act.wait_ge(v_ok, BATCH)

        def act_steps(base, first=False, last=False):
            for s in range(4):
                g = base + s
                for kt in range(TT):
                    for j in range(REP):
                        act.wait_ge(t_mm, 16 * g + 4 * kt + j + 1)
                        if j == 0:
                            positive(act, pv_mm, 4 * g + kt - 1)
                        nc.scalar.activation(probs[kt % 2][:, j, :], BANK[4 + j % 2], ACT.Exp,
                                             scale=HEAD_DIM ** -0.5).then_inc(exp_ok, 1)
                        if kt == 1 and j == 0 and not (first and s == 0):
                            copy_u(g - 1)

        def copy_u(g):
            act.wait_ge(pv_mm, 4 * g + 4)
            positive(act, uT_ok, g)
            nc.scalar.activation(u_sb[:], BANK[6], ACT.Copy).then_inc(u_ok, 1)

        act_steps(0, first=True)
        with act.Fori(1, GROUPS // 4 - 1) as i:
            act_steps(4 * i)
        act_steps(GROUPS - 4, last=True)
        copy_u(LAST_G)

        act.wait_ge(att_out[0], 16 * GROUPS // 2)
        act.wait_ge(att_out[1], 16 * GROUPS // 2)
        def hi_attended(b, kt):
            act.wait_ge(aT_ok, 4 * b + kt + 1)
            positive(act, o_mm, 4 * b)
            nc.scalar.activation(ah[:, kt, :], BANK[6 + kt % 2], ACT.Copy).then_inc(ah_ok, 1)

        def hi_norm(b, kt):
            act.wait_ge(x2T_mm, 4 * b + kt + 1)
            positive(act, u_mm, IT * b)
            nc.scalar.activation(fxh[:, kt, :], BANK[NORM_BANK[kt]], ACT.Copy).then_inc(fxh_ok, 1)

        def weights_out(e):
            for k, dst in enumerate((w1T, w3T, w2T)):
                act.wait_ge(wT_mm, 3 * e + k + 1)
                nc.scalar.activation(dst[:, e, :], BANK[3 * (e % 2) + k], ACT.Copy).then_inc(wT_ok, 1)

        for e in range(IT):
            act.wait_ge(d_ok, e + 1)
            nc.scalar.activation(wn[e % RING][:], wn[e % RING][:], ACT.Sign).then_inc(sg_ok, 1)
            if e > 0:
                weights_out(e - 1)
            if e < KT:
                hi_attended(0, e)
        weights_out(IT - 1)
        for kt in range(KT):
            hi_norm(0, kt)
        def hi_gate_up(n, src, parity):
            if n is not None:
                act.wait_ge(u_mm, n - 1)
            for k, w in enumerate((w1T, w3T)):
                nc.scalar.activation(wh[parity][:, k, :], w[:, bass.ds(src, 1), :].rearrange("p o c -> p (o c)"),
                                     ACT.Copy).then_inc(wh_ok, 1)

        def act_tile(b, e, nxt, p):
            n = IT * b + e
            act.wait_ge(g_mm, n + 1)
            act.wait_ge(hl_ok, CREDIT + n)
            nc.scalar.activation(gate[:], BANK[GATE], ACT.Silu).then_inc(silu_ok, 1)
            act.wait_ge(h_ok, CREDIT + n + 1)
            act.wait_ge(d_mm, CREDIT + n - 1)
            nc.scalar.activation(hh[p][:], gate[:], ACT.Copy).then_inc(hh_ok, 1)
            if nxt is not None:
                hi_gate_up(n + 2, nxt, p)

        act.wait_ge(wT_ok, 3 * IT)
        for p in range(2):
            hi_gate_up(None, p, p)
        with act.Fori(0, BATCH - 1) as b:
            for e in range(IT):
                act_tile(b, e, (e + 2) % IT, e % 2)
                if LAG <= e < LAG + KT:
                    hi_attended(b + 1, e - LAG)
            for kt in range(KT):
                hi_norm(b + 1, kt)
        with act.Fori(0, IT // 2 - 1) as i:
            for p in range(2):
                act_tile(BATCH - 1, 2 * i + p, 2 * i + p + 2, p)
        for e in range(IT - 2, IT):
            act_tile(BATCH - 1, e, None, e % 2)

    @block.vector
    def _(dve):
        dve.nop(nofuse=True).then_inc(h_ok, CREDIT)
        dve.nop(nofuse=True).then_inc(hl_ok, CREDIT)
        dve.nop(nofuse=True).then_inc(res_ok, CREDIT)
        v = nc.vector
        chain = Chain(dve, dve_ch)

        for n, (t0, tiles) in enumerate(((QT, 4), (KTILE, 2), (OT, 4))):
            dve.wait_ge(w_in[n], (16, 32, 16)[n])
            chain.link(v.tensor_reduce(wstat[:, 0, t0:t0 + tiles], w_nat[:, t0:t0 + tiles, :], AX.X, ALU.add,
                                       apply_absolute_value=True))
        chain.link(v.tensor_scalar(wstat[:, 1, :], wstat[:, 0, :], 1.0 / HID, 1e-8, ALU.mult, ALU.max))
        v.reciprocal(wstat[:, 2, :], wstat[:, 1, :]).then_inc(wstat_ok, 1)
        dve.wait_ge(scl_in, 64)
        chain.link(v.tensor_tensor(wstat[:, 5, :], wstat[:, 1, :], scl[:], ALU.mult))
        v.tensor_scalar(wstat[:, 3, :], wstat[:, 5, :], -FLT_MAX, FLT_MAX, ALU.max, ALU.min).then_inc(wstat_ok, 1)
        chain.link(v.tensor_scalar(wstat[:, 0, :], wstat[:, 5, :], 0.0, 0.0, ALU.mult, ALU.is_equal))
        v.tensor_scalar(wstat[:, 4, :], wstat[:, 0, :], -1.0, 1.0, ALU.mult, ALU.add).then_inc(wstat_ok, 1)

        for t in range(NT):
            dve.wait_ge(x_in[t // TT], 16)
            v.bn_stats(stats[:, t, :], x_sb[:, t, :]).then_inc(stat_ch, 1)
        for t in range(NT):
            dve.wait_ge(stat_ch, NT)
            v.bn_aggr(mv[:, t, :], stats[:, t, :]).then_inc(stat_ch, 1)
        dve.wait_ge(stat_ch, 2 * NT)
        v.tensor_scalar(ve[:], mv[:, :, 1], EPS, None, ALU.add).then_inc(stat_ch, 1)

        for m in range(WTILES):
            dve.wait_ge(sgnT_ok, m + 1)
            dst = signs[:, :, m * P:(m + 1) * P] if m < OT else signs_o[:, :, (m - OT) * P:(m - OT + 1) * P]
            src = BANK[m % 4].bitcast(BF16)[:, 0:HID].rearrange("p (t c) -> p t c", c=P)
            v.tensor_copy(dst, src).then_inc(signs_ok, 1)
        dve.wait_ge(rstd_ok, 1)
        dve.wait_ge(fac_in, 32)

        def norm(i, p):
            for t in range(TT):
                tile = 4 * (2 * i + p) + t
                dve.wait_ge(xT_ok[p], 4 * i)
                v.tensor_scalar(xn[p][:, t, :], x_sb[:, bass.ds(tile, 1), :].rearrange("p o c -> p (o c)"),
                                mv[:, bass.ds(tile, 1), 0:1].rearrange("p o c -> p (o c)"),
                                rstd[:, bass.ds(tile, 1)], ALU.subtract, ALU.mult).then_inc(xn_ok[p], 1)

        with dve.Fori(0, 2) as i:
            chain.enter(i, 2 * (5 + 2))
            for p in range(2):
                norm(i, p)
            for p in range(2):
                for kt in range(KT):
                    dve.wait_ge(xh_ok[p], 4 * i + kt + 1)
                    v.tensor_tensor(xl[p][:, kt, :], BANK[kt], xh[p][:, kt, :].bitcast(FP32),
                                    ALU.subtract).then_inc(xl_ok[p], 1)
            for p in range(2):
                b = 2 * i + p
                for m in range(5):
                    y = yq[p][:, m, :]
                    dve.wait_ge(yq_ok, 5 * b + m + 1)
                    dve.wait_ge(ql_ok, 5 * b + m)
                    if m == 0:
                        dve.wait_ge(v_ok, b)
                    v.tensor_scalar(g_alt[:], y, GUARD, -GUARD, ALU.min, ALU.max)
                    chain.link(v.tensor_scalar(g_mask[:], y, wstat[:, 4, m:m + 1], 0.0, ALU.mult, ALU.is_equal))
                    settle(dve)
                    v.copy_predicated(g_alt[:], g_mask[:], y).then_inc(yg_ok, 1)
                    dve.wait_ge(qh_ok, 5 * b + m + 1)
                    v.tensor_tensor(q_lo[:, m, :], g_alt[:], q_hi[:, m, :].bitcast(FP32), ALU.subtract).then_inc(ql_ok, 1)
                row = [fac_row[:, a, 0, :].unsqueeze(1).to_broadcast([P, TT, P]) for a in range(2)]
                alt = g_alt[:].rearrange("p (t c) -> p t c", c=P)
                mask = g_mask[:].rearrange("p (t c) -> p t c", c=P)
                dve.wait_ge(v_mm[p], i + 1)
                v.tensor_tensor(vy[:], BANK[7].rearrange("p (t c) -> p t c", c=P), row[0], ALU.mult).then_inc(vy_ok, 1)
                dve.wait_ge(vy_ok, b + 1)
                dve.wait_ge(ql_ok, 5 * (b + 1))
                v.tensor_scalar(alt, vy[:], GUARD, -GUARD, ALU.min, ALU.max)
                chain.link(v.scalar_tensor_tensor(mask, vy[:], 0.0, row[1], ALU.mult, ALU.is_equal))
                settle(dve)
                chain.link(v.copy_predicated(alt, mask, vy[:]))
                for kv in range(KV_HEADS):
                    last = v.tensor_copy(v_sb[:, bass.ds(8 * b + kv, 1), :, :].rearrange("p o t d -> p (o t) d"),
                                         alt[:, :, kv * HEAD_DIM:(kv + 1) * HEAD_DIM])
                last.then_inc(v_ok, 1)
            chain.leave(2)

        for m in range(5):
            dve.wait_ge(part_out[m], BATCH * 64)
        for s in range(4):
            v.memset(k_slot[s][SHIFT_ROW:STACK].bitcast(FP32), 0.0).then_inc(slot_init, 1)
        dve.wait_ge(slot_init, 8)
        for s in range(4):
            v.memset(k_slot[s][SHIFT_ROW:SHIFT_ROW + 2].bitcast(FP32), 1.0).then_inc(slot_init, 1)
        for s in range(2):
            v.memset(v_slot[s][:, :, HEAD_DIM:], 1.0).then_inc(slot_init, 1)

        def maxima(base, nn):
            rel, j, half_tile = nn // 8, nn % 8 // 2, nn % 2
            c = j * TT + 2 * half_tile
            dve.wait_ge(s_mm, 8 * base + nn + 1)
            pair = psum[:, 2 * half_tile:2 * half_tile + 2, :]
            v.tensor_reduce(nmx[rel % 2][:, c:c + 2], pair, AX.X, ALU.max, negate=True).then_inc(s_max, 1)

        def split_shift(g, s, reused):
            dve.wait_ge(mT_ok, g + 1)
            if reused is not None:
                dve.wait_ge(shift_in[(s + 2) % 4], reused)
            src = BANK[7][0:REP * TT, 0:P]
            v.tensor_scalar(shift[s % 2][:, 0, :], src, -SHIFT_MAX, SHIFT_MAX, ALU.max, ALU.min).then_inc(sh_hi, 1)
            dve.wait_ge(sh_hi, g + 1)
            v.scalar_tensor_tensor(shift[s % 2][:, 1, :], src, -SHIFT_MAX, shift[s % 2][:, 0, :].bitcast(FP32),
                                   ALU.max, ALU.subtract).then_inc(sh_lo, 1)

        def normalise(g, s, reused):
            u = BANK[7].rearrange("p (n c) -> p n c", c=32)
            dve.wait_ge(uT_ok, g + 1)
            v.reciprocal(u_rec[:], u[:, :, HEAD_DIM]).then_inc(rec_ok, 1)
            dve.wait_ge(rec_ok, g + 1)
            if reused is not None:
                dve.wait_ge(att_out[s % 2], reused)
            v.tensor_tensor(att[s % 2][:].rearrange("p t (j d) -> p (t j) d", d=HEAD_DIM), u[:, :, 0:HEAD_DIM],
                            u_rec[:].unsqueeze(2).to_broadcast([P, REP * TT, HEAD_DIM]), ALU.mult
                            ).then_inc(att_ok, 1)

        def dve_steps(i, first=False, last=False):
            base = 4 * i
            for s in range(4):
                g = base + s
                for kt in range(TT):
                    for a in range(2):
                        nn = 8 * s + 2 * kt + a + S_AHEAD
                        if not (last and nn >= 32):
                            maxima(base, nn)
                        if s % 2 == 1 and kt == 2 and a == 1 and not last:
                            dve.wait_ge(fd_ok, 2 * i + s // 2 + 1)
                            v.tensor_reduce(dsum[:, :, bass.ds(2 * i + s // 2, 1)], fw[s // 2][:], AX.X, ALU.add,
                                            apply_absolute_value=True).then_inc(fsum_ok, 1)
                        if kt == 2 and a == 0 and not (last and s == 3):
                            n = s + 1
                            reused = None if first and s == 0 else 32 * i + (32 if n >= 2 else 0)
                            split_shift(g + 1, n % 4, reused)
                        if kt == 3 and a == 0 and not (first and s == 0):
                            reused = None if first and s < 3 else 16 * (2 * i) + 16 * ((s - 3) // 2 + 1)
                            normalise(g - 1, (s + 3) % 4, reused)

        for nn in range(S_AHEAD):
            maxima(0, nn)
            if nn == 8:
                split_shift(0, 0, None)
        dve_steps(0, first=True)
        with dve.Fori(1, GROUPS // 4 - 1) as i:
            dve_steps(i)
        dve_steps(GROUPS // 4 - 1, last=True)
        normalise(LAST_G, 3, 16 * (GROUPS // 2 - 1))

        for p in range(2):
            dve.wait_ge(att_out[p], 16 * GROUPS // 2)
        def lo_attended(b, kt):
            dve.wait_ge(ah_ok, 4 * b + kt + 1)
            v.tensor_tensor(al[:, kt, :], BANK[6 + kt % 2], ah[:, kt, :].bitcast(FP32), ALU.subtract).then_inc(al_ok, 1)

        def lo_norm(b, kt):
            dve.wait_ge(fxh_ok, 4 * b + kt + 1)
            v.tensor_tensor(fxl[:, kt, :], BANK[NORM_BANK[kt]], fxh[:, kt, :].bitcast(FP32), ALU.subtract
                            ).then_inc(fxl_ok, 1)

        def residual(b, t, chain):
            row = [fac_row[:, a, OT - VTILE:OT - VTILE + KT, :].rearrange("p t c -> p (t c)") for a in range(2)]
            y = oy[:]
            dve.wait_ge(o_mm, 4 * b + t + 1)
            v.tensor_tensor(y, BANK[6 + t % 2], row[0], ALU.mult).then_inc(oy_ok, 1)
            dve.wait_ge(oy_ok, 4 * b + t + 1)
            chain.link(v.tensor_tensor(o_alt[:], y, y, ALU.is_equal))
            chain.link(v.scalar_tensor_tensor(o_alt[:], o_alt[:], GUARD, y, ALU.mult, ALU.min))
            v.tensor_scalar(o_alt[:], o_alt[:], -GUARD, None, ALU.max)
            chain.link(v.scalar_tensor_tensor(o_mask[:], y, 0.0, row[1], ALU.mult, ALU.is_equal))
            settle(dve)
            chain.link(v.copy_predicated(o_alt[:], o_mask[:], y))
            if t == 0:
                dve.wait_ge(x_again, 16 * (b + 1))
            v.tensor_tensor(x1[:, t, :], x1[:, t, :], o_alt[:], ALU.add).then_inc(x1_ok, 1)
            dve.wait_ge(x1_ok, 4 * b + t + 1)
            chain.link(v.bn_stats(st2[:, t, :], x1[:, t, :]))

        def second_norm(b, chain):
            settle(dve)
            for t in range(TT):
                last = v.bn_aggr(mv2[:, t, :], st2[:, t, :])
            chain.link(last)
            v.tensor_scalar(ve2[:], mv2[:, :, 1], EPS, None, ALU.add).then_inc(ve2_ok, 1)
            dve.wait_ge(rstd2_ok, b + 1)
            dve.wait_ge(aT_ok, 4 * (b + 1))
            for t in range(TT):
                v.tensor_scalar(an[:, t, :], x1[:, t, :], mv2[:, t, 0:1], rstd2[:, t:t + 1],
                                ALU.subtract, ALU.mult).then_inc(xn2_ok, 1)

        dve.wait_ge(fsum_ok, IT)
        v.tensor_reduce(dtot[:], dsum[:], AX.X, ALU.add).then_inc(dtot_ok, 1)
        dve.wait_ge(ctot_mm, 1)
        v.tensor_scalar(coeff[:], BANK[5][:, 0:3], 1.0 / (INTER * HID), None, ALU.mult).then_inc(coeff_ok, 1)
        dve.wait_ge(coeff_ok, 1)
        per_batch = TT * 5 + 1
        c_chain = Chain(dve, c_ch)
        for e in range(IT):
            slot = e % RING
            dve.wait_ge(sg_ok, e + 1)
            for k in range(3):
                v.scalar_tensor_tensor(wn[slot][:, k, :], wn[slot][:, k, :], coeff[:, k:k + 1], mn[slot][:, k, :],
                                       ALU.mult, ALU.add).then_inc(w_ok, 1)
            if e < KT:
                lo_attended(0, e)
            elif e < KT + TT:
                residual(0, e - KT, c_chain)
            elif e == NORM_STEP:
                second_norm(0, c_chain)
        for kt in range(KT):
            lo_norm(0, kt)

        def lo_gate_up(done, src, parity):
            for k, w in enumerate((w1T, w3T)):
                dve.wait_ge(wh_ok, done + k + 1)
                v.tensor_tensor(wl[parity][:, k, :], w[:, bass.ds(src, 1), :].rearrange("p o c -> p (o c)"),
                                wh[parity][:, k, :].bitcast(FP32), ALU.subtract).then_inc(wl_ok, 1)

        def dve_tile(b, e, src, nxt, p):
            n = IT * b + e
            dve.wait_ge(silu_ok, CREDIT + n + 1)
            dve.wait_ge(u_mm, n + 1)
            v.tensor_tensor(gate[:], gate[:], BANK[UP], ALU.mult).then_inc(h_ok, 1)
            dve.wait_ge(hh_ok, n + 1)
            v.tensor_tensor(hl[p][:], gate[:], hh[p][:].bitcast(FP32), ALU.subtract).then_inc(hl_ok, 1)
            dve.wait_ge(dh_ok, n + 1)
            v.tensor_tensor(dl[p][:], w2T[:, bass.ds(src, 1), :].rearrange("p o c -> p (o c)"),
                            dh[p][:].bitcast(FP32), ALU.subtract).then_inc(dl_ok, 1)
            if nxt is not None:
                lo_gate_up(2 * (n + 2), nxt, p)

        def results(b):
            dve.wait_ge(d_mm, CREDIT + IT * (b + 1))
            dve.wait_ge(res_in, 16 * (b + 1))
            for t in range(TT):
                v.tensor_tensor(res[:, t, :], BANK[DOWN + t], res[:, t, :], ALU.add).then_inc(res_ok, 1)

        for p in range(2):
            lo_gate_up(2 * p, p, p)
        with dve.Fori(0, BATCH - 1) as b:
            c_chain.enter(b, per_batch)
            for e in range(IT):
                dve_tile(b, e, e, (e + 2) % IT, e % 2)
                if LAG <= e < LAG + KT:
                    lo_attended(b + 1, e - LAG)
                elif LAG + KT <= e < LAG + KT + TT:
                    residual(b + 1, e - LAG - KT, c_chain)
                elif e == LAG + NORM_STEP:
                    second_norm(b + 1, c_chain)
            for kt in range(KT):
                lo_norm(b + 1, kt)
            results(b)
            c_chain.leave(BATCH - 1)
        with dve.Fori(0, IT // 2 - 1) as i:
            for p in range(2):
                dve_tile(BATCH - 1, 2 * i + p, 2 * i + p, 2 * i + p + 2, p)
        for e in range(IT - 2, IT):
            dve_tile(BATCH - 1, e, e, None, e % 2)
        results(BATCH - 1)

    @block.tensor
    def _(pe):
        pe.nop(nofuse=True).then_inc(d_mm, CREDIT)
        mm, tr = nc.tensor.matmul, nc.tensor.transpose
        pe.wait_ge(const_ok, 5)
        for m in range(WTILES):
            pe.wait_ge(sgn_ok, m + 1)
            positive(pe, signs_ok, m - 3)
            for kt in range(KT):
                last = tr(BANK[m % 4].bitcast(BF16)[:, kt * P:(kt + 1) * P], w_sgn[:, m, kt * P:(kt + 1) * P], ident16[:])
            last.then_inc(sgnT_ok, 1)
        pe.wait_ge(signs_ok, WTILES)

        with pe.Fori(0, 2) as i:
            for p in range(2):
                pe.wait_ge(xn_ok[p], 4 * (i + 1))
                pe.wait_ge(xl_ok[1 - p], 4 * (i + p))
                for kt in range(KT):
                    for t in range(TT):
                        last = tr(BANK[kt][:, t * P:(t + 1) * P], xn[p][:, t, kt * P:(kt + 1) * P], ident[:])
                    last.then_inc(xT_ok[p], 1)
            for p in range(2):
                b = 2 * i + p
                pe.wait_ge(xl_ok[p], 4 * (i + 1))
                for m in range(5):
                    pe.wait_ge(yq_ok, 5 * b + max(m - 2, 0))
                    w = slice(m * P, (m + 1) * P)
                    for kt in range(KT):
                        mm(BANK[4 + m % 3], signs[:, kt, w], xh[p][:, kt, :], start=(kt == 0), stop=False)
                        last = mm(BANK[4 + m % 3], signs[:, kt, w], xl[p][:, kt, :], start=False, stop=(kt == KT - 1))
                    last.then_inc(q_mm, 1)
                pe.wait_ge(vy_ok, b)
                w = slice(VTILE * P, (VTILE + 1) * P)
                for t in range(TT):
                    o = BANK[7][:, t * P:(t + 1) * P]
                    for kt in range(KT):
                        mm(o, xh[p][:, kt, t * P:(t + 1) * P], signs[:, kt, w], start=(kt == 0), stop=False)
                        last = mm(o, xl[p][:, kt, t * P:(t + 1) * P], signs[:, kt, w], start=False, stop=(kt == KT - 1))
                last.then_inc(v_mm[p], 1)

        pe.wait_ge(v_ok, BATCH)
        pe.wait_ge(slot_init, 14)

        def scores(i, nn):
            rel, j, half_tile = nn // 8, nn % 8 // 2, nn % 2
            s = rel % 4
            if nn % 8 == 0:
                pe.wait_ge(slot_in[s], 48 * (i + rel // 4 + 1))
                positive(pe, cleared, 4 * i + rel - 3)
            positive(pe, s_max, 32 * i + nn - 1)
            for a in range(2):
                q = 2 * half_tile + a
                last = mm(BANK[q], q_slot[s][:, j, q * P:(q + 1) * P], k_slot[s][:], start=True, stop=True)
            last.then_inc(s_mm, 1)

        def transpose_maxima(g, s, before):
            pe.wait_ge(s_max, 8 * g + 8)
            positive(pe, att_ok, before)
            tr(BANK[7][0:REP * TT, 0:P], nmx[s % 2][:], ident[:]).then_inc(mT_ok, 1)

        def shifted_scores(i, s, kt, j):
            g = 4 * i + s
            if kt == 0 and j == 0:
                pe.wait_ge(shift_in[s], 32 * (i + 1))
            positive(pe, exp_ok, 16 * g + 4 * kt + j - 1)
            mm(BANK[4 + j % 2], k_slot[s][:, kt * P:(kt + 1) * P], q_slot[s][:, j, :],
               start=True, stop=True).then_inc(t_mm, 1)

        def weigh_values(g, s, kt):
            pe.wait_ge(exp_ok, 16 * g + 4 * kt + 4)
            if kt == 0:
                pe.wait_ge(vs_ok, g + 1)
                positive(pe, u_ok, g)
            for j in range(REP):
                last = mm(psum[32 * j:32 * j + 32, 6, :], v_slot[s % 2][:, kt, :], probs[kt % 2][:, j, :],
                          start=(kt == 0), stop=(kt == TT - 1))
            last.then_inc(pv_mm, 1)

        def transpose_values(g, lows):
            pe.wait_ge(u_ok, g + 1)
            pe.wait_ge(sh_lo, lows)
            for t in range(TT):
                last = tr(BANK[7][:, t * P:(t + 1) * P], u_sb[:, t * P:(t + 1) * P], ident[:])
            last.then_inc(uT_ok, 1)

        def pe_steps(i, first=False, last=False):
            for s in range(4):
                g = 4 * i + s
                for kt in range(TT):
                    for j in range(REP):
                        shifted_scores(i, s, kt, j)
                        nn = 8 * s + 2 * kt + j // 2 + S_AHEAD
                        if j % 2 == 1 and not (last and nn >= 32):
                            scores(i, nn)
                    if kt > 0:
                        weigh_values(g, s, kt - 1)
                    elif not (first and s == 0):
                        weigh_values(g - 1, s + 3, TT - 1)
                    if kt == 1 and not (last and s == 3):
                        transpose_maxima(g + 1, s + 1, g - 1)
                    if kt == 2 and last and s == 3:
                        pe.wait_ge(att_ok, g - 1)
                    if kt == 2 and not (first and s == 0):
                        transpose_values(g - 1, g + 1 if last and s == 3 else g + 2)

        for nn in range(S_AHEAD):
            scores(0, nn)
            if nn == 8:
                transpose_maxima(0, 0, 0)
        pe_steps(0, first=True)
        with pe.Fori(1, GROUPS // 4 - 1) as i:
            pe_steps(i)
        pe_steps(GROUPS // 4 - 1, last=True)
        weigh_values(LAST_G, 3, TT - 1)
        pe.wait_ge(att_ok, LAST_G)
        transpose_values(LAST_G, GROUPS)

        def transpose_attended(b, kt):
            if kt == 0:
                pe.wait_ge(an_in, 32 * (b + 1))
                positive(pe, fxl_ok, 4 * b)
            if kt >= 2:
                pe.wait_ge(al_ok, 4 * b + kt - 1)
            for t in range(TT):
                last = tr(BANK[6 + kt % 2][:, t * P:(t + 1) * P], an[:, t, kt * P:(kt + 1) * P], ident[:])
            last.then_inc(aT_ok, 1)

        def project(b, t):
            if t == 0:
                pe.wait_ge(al_ok, 4 * (b + 1))
            if t >= 2:
                pe.wait_ge(oy_ok, 4 * b + t - 1)
            for kt in range(KT):
                mm(BANK[6 + t % 2], ah[:, kt, t * P:(t + 1) * P], signs_o[:, kt, :], start=(kt == 0), stop=False)
                last = mm(BANK[6 + t % 2], al[:, kt, t * P:(t + 1) * P], signs_o[:, kt, :],
                          start=False, stop=(kt == KT - 1))
            last.then_inc(o_mm, 1)

        def transpose_norm(b, kt):
            if kt == 0:
                pe.wait_ge(xn2_ok, 4 * (b + 1))
                pe.wait_ge(oy_ok, 4 * (b + 1))
            if kt >= 2:
                if not isinstance(b, int):
                    pe.wait_ge((silu_ok, h_ok)[kt - 2], CREDIT + IT * b)
            for t in range(TT):
                last = tr(BANK[NORM_BANK[kt]][:, t * P:(t + 1) * P], an[:, t, kt * P:(kt + 1) * P], ident[:])
            last.then_inc(x2T_mm, 1)

        pe.wait_ge(att_ok, GROUPS)
        pe.wait_ge(dtot_ok, 1)
        mm(BANK[5][:, 0:3], ones[:], dtot[:], start=True, stop=True).then_inc(ctot_mm, 1)
        for e in range(IT):
            if e < KT:
                transpose_attended(0, e)
            elif e < KT + TT:
                project(0, e - KT)
            for k in range(3):
                pe.wait_ge(w_ok, 3 * e + k + 1)
                if e >= 2:
                    pe.wait_ge(wT_ok, 3 * (e - 2) + k + 1)
                for t in range(TT):
                    last = tr(BANK[3 * (e % 2) + k][:, t * P:(t + 1) * P], wn[e % RING][:, k, t * P:(t + 1) * P], ident[:])
                last.then_inc(wT_mm, 1)
        pe.wait_ge(wT_ok, 3 * (IT - 1))
        for kt in range(KT):
            transpose_norm(0, kt)
        pe.wait_ge(wT_ok, 3 * IT)

        def three(o, lhs_hi, lhs_lo, rhs_hi, rhs_lo, first, final):
            mm(o, lhs_hi, rhs_hi, start=first, stop=False)
            mm(o, lhs_hi, rhs_lo, start=False, stop=False)
            return mm(o, lhs_lo, rhs_hi, start=False, stop=final)

        def gate_up(n, p, start=None):
            for k, (bank, used, done) in enumerate(((GATE, silu_ok, g_mm), (UP, h_ok, u_mm))):
                pe.wait_ge(wl_ok, 2 * n + k + 1)
                pe.wait_ge(used, CREDIT + n)
                for kt in range(KT):
                    c = slice(kt * P, (kt + 1) * P)
                    last = three(BANK[bank], wh[p][:, k, c], wl[p][:, k, c], fxh[:, kt, :], fxl[:, kt, :],
                                 kt == 0, kt == KT - 1)
                last.then_inc(done, 1)

        def down(n, p, first, final):
            pe.wait_ge(dl_ok, n + 1)
            pe.wait_ge(hl_ok, CREDIT + n + 1)
            for t in range(TT):
                c = slice(t * P, (t + 1) * P)
                last = three(BANK[DOWN + t], hh[p][:, c], hl[p][:, c], dh[p][:], dl[p][:], first, final)
            last.then_inc(d_mm, 1)

        with pe.Fori(0, BATCH - 1) as b:
            pe.wait_ge(fxl_ok, 4 * (b + 1))
            for e in range(IT):
                gate_up(IT * b + e, e % 2)
                if e == 1:
                    pe.wait_ge(res_ok, CREDIT + 4 * b)
                if e > 0:
                    down(IT * b + e - 1, (e - 1) % 2, e == 1, False)
                if LAG <= e < LAG + KT:
                    transpose_attended(b + 1, e - LAG)
                elif LAG + KT <= e < LAG + KT + TT:
                    project(b + 1, e - LAG - KT)
            for kt in range(KT):
                transpose_norm(b + 1, kt)
            down(IT * (b + 1) - 1, 1, False, True)
        n = IT * (BATCH - 1)
        pe.wait_ge(fxl_ok, 4 * BATCH)
        gate_up(n, 0)
        gate_up(n + 1, 1)
        pe.wait_ge(res_ok, CREDIT + 4 * (BATCH - 1))
        down(n, 0, True, False)
        with pe.Fori(1, IT // 2) as i:
            for p in range(2):
                gate_up(n + 2 * i + p, p)
                down(n + 2 * i + p - 1, 1 - p, False, False)
        down(IT * BATCH - 1, 1, False, True)

    ctx.close()


_INS = ["L0_attn_hidden_states", "L0_attn_q_weight", "L0_attn_q_scale", "L0_attn_k_weight", "L0_attn_k_scale",
        "L0_attn_v_weight", "L0_attn_v_scale", "L0_attn_o_weight", "L0_attn_o_scale",
        "L0_ffn_w1", "L0_ffn_mean_w1", "L0_ffn_w2", "L0_ffn_mean_w2", "L0_ffn_w3", "L0_ffn_mean_w3"]
_OUTS = [((BATCH, SEQ, HID), "float32")]


def kernel(**inputs):
    import numpy as _np
    import concourse.bacc as _bacc
    from concourse import mybir as _mybir
    from concourse.bass_utils import run_bass_kernel_spmd as _run

    nc = _bacc.Bacc("TRN2", target_bir_lowering=False, num_devices=1)
    arrays, args = {}, []
    for name in _INS:
        a = _np.ascontiguousarray(inputs[name])
        arrays[f"in_{name}_dram"] = a
        args.append(nc.dram_tensor(f"in_{name}_dram", a.shape, _mybir.dt.from_np(a.dtype), kind="ExternalInput").ap())
    for i, (shape, dtype) in enumerate(_OUTS):
        dt = _mybir.dt.from_np(_np.dtype(dtype))
        args.append(nc.dram_tensor(f"out_{i}_dram", shape, dt, kind="ExternalOutput").ap())
    decoder_layer(nc, *args)
    r = _run(nc, [arrays], core_ids=[0])
    return r.results[0]["out_0_dram"]
```

```python
import numpy as np
import concourse.bass as bass
from concourse import mybir
from contextlib import ExitStack

FP32 = mybir.dt.float32
FP32R = mybir.dt.float32r
BF16 = mybir.dt.bfloat16
I32 = mybir.dt.int32
I8 = mybir.dt.int8
ALU = mybir.AluOpType
ACT = mybir.ActivationFunctionType
AX = mybir.AxisListType

P = 128
BATCH, SEQ, HID = 4, 512, 512
HEADS, KV_HEADS = 32, 8
HEAD_DIM = HID // HEADS
REP = HEADS // KV_HEADS
GROUPS = BATCH * KV_HEADS
INTER = 1792
KT = HID // P
TT = SEQ // P
NT = BATCH * TT
IT = INTER // P
QT, KTILE, VTILE, OT = 0, 4, 5, 6
WTILES = 10
BIT_IN = 768
EPS = 1e-5
FLT_MAX = float(np.finfo(np.float32).max)
GUARD = 1e6
SHIFT_MAX = 3e38
STACK = 96
SHIFT_ROW = 64


def positive(eng, sem, value):
    if not isinstance(value, int) or value > 0:
        eng.wait_ge(sem, value)


def settle(eng):
    eng.nop(nofuse=True)


Y_RING = 4
RING = 4


class Chain:

    def __init__(self, eng, sem):
        self.eng, self.sem, self.base, self.k, self.saved = eng, sem, 0, 0, 0

    def link(self, ins):
        ins.then_inc(self.sem, 1)
        self.k += 1
        self.eng.wait_ge(self.sem, self.base + self.k)

    def enter(self, i, per):
        self.saved, self.per = self.base + self.k, per
        self.base, self.k = self.saved + i * per, 0

    def leave(self, times):
        assert self.k == self.per, (self.k, self.per)
        self.base, self.k = self.saved + times * self.per, 0


def decoder_layer(nc, x, q_w, q_s, k_w, k_s, v_w, v_s, o_w, o_s, w1, m1, w2, m2, w3, m3, out):
    ctx = ExitStack()

    def sem(name):
        return ctx.enter_context(nc.semaphore(name))

    def sems(name, n):
        return [sem(f"{name}{i}") for i in range(n)]

    def region(scope):
        return lambda name, shape, dt=FP32: scope.enter_context(nc.sbuf_tensor(name, shape, dt))

    q_dram = nc.dram_tensor("q_parts", [GROUPS, 2, HEAD_DIM, REP, SEQ], FP32, kind="Internal").ap()
    k_dram = nc.dram_tensor("k_stack", [GROUPS, 4 * HEAD_DIM, SEQ], FP32, kind="Internal").ap()
    fac_dram = nc.dram_tensor("factors", [2, WTILES, P], FP32, kind="Internal").ap()
    u_dram = nc.dram_tensor("weighted_values", [BATCH, KT, 2 * REP, 2 * HEAD_DIM, SEQ], FP32, kind="Internal").ap()
    rec_dram = nc.dram_tensor("reciprocals", [BATCH, HEADS, SEQ], FP32, kind="Internal").ap()
    x1_dram = nc.dram_tensor("residual", [NT, P, HID], FP32, kind="Internal").ap()

    keep = region(ctx)
    ident = keep("ident", [P, P])
    ident16 = keep("ident16", [P, P], BF16)
    half = keep("minus_half", [P, NT])
    ones = keep("ones", [P, P])
    signs_o = keep("signs_o", [P, KT, HID], FP32R)
    fac_row = keep("fac_row", [P, 2, KT, P])
    dsum = keep("dsum", [P, 3, IT])
    dtot = keep("dtot", [P, 3])
    coeff = keep("coeff", [P, 3])
    until_c = ExitStack()
    mid = region(until_c)
    stage = [mid(f"stage{p}", [P, 3, HID]) for p in range(RING)]
    wn, mn = stage[0::2], stage[1::2]
    v_sb = mid("v_sb", [P, GROUPS, TT, HEAD_DIM])

    with ExitStack() as scope:
        sb = region(scope)
        x_sb = sb("x_sb", [P, NT, HID])
        w_sgn = sb("w_sgn", [P, WTILES, HID], BF16)
        w_nat = sb("w_nat", [P, WTILES, HID])
        signs = sb("signs_qkv", [P, KT, BIT_IN], FP32R)
        scl = sb("scl", [P, WTILES])
        wstat = sb("wstat", [P, 6, WTILES])
        stats = sb("stats", [P, NT, 6])
        mv = sb("mv", [P, NT, 2])
        ve = sb("ve", [P, NT])
        rstd = sb("rstd", [P, NT])
        xn = [sb(f"xn{p}", [P, TT, HID]) for p in range(2)]
        xh = [sb(f"xh{p}", [P, KT, SEQ], FP32R) for p in range(2)]
        xl = [sb(f"xl{p}", [P, KT, SEQ], FP32R) for p in range(2)]
        yq = [w_nat[:, n, :] for n in range(Y_RING)]
        q_hi = sb("q_hi", [P, 5, SEQ], FP32R)
        q_lo = sb("q_lo", [P, 5, SEQ], FP32R)
        g_mask = [sb(f"g_mask{p}", [P, SEQ], I32) for p in range(2)]
        g_alt = [sb(f"g_alt{p}", [P, SEQ]) for p in range(2)]
    with ExitStack() as scope:
        sb = region(scope)
        q_slot = [sb(f"q_slot{s}", [STACK, REP, SEQ], FP32R) for s in range(4)]
        k_slot = [sb(f"k_slot{s}", [STACK, SEQ], FP32R) for s in range(4)]
        v_slot = [sb(f"v_slot{s}", [P, TT, 32]) for s in range(2)]
        nmx = [sb(f"nmx{s}", [P, REP * TT]) for s in range(2)]
        shift = [sb(f"shift{s}", [REP * TT, 2, P], FP32R) for s in range(2)]
        probs = [sb(f"probs{s}", [P, REP, SEQ]) for s in range(TT)]
        u_sb = [sb(f"u_sb{s}", [P, SEQ]) for s in range(2)]
    until_c.close()
    late = region(ctx)
    wh = [late(f"wh{p}", [P, 2, HID], FP32R) for p in range(2)]
    wl = [late(f"wl{p}", [P, 2, HID], FP32R) for p in range(2)]
    dh = [late(f"dh{p}", [P, HID], FP32R) for p in range(2)]
    dl = [late(f"dl{p}", [P, HID], FP32R) for p in range(2)]
    w1T = late("w1T", [P, IT, HID])
    w3T = late("w3T", [P, IT, HID])
    w2T = late("w2T", [P, IT, HID])
    fxh = late("fxh", [P, KT, SEQ], FP32R)
    fxl = late("fxl", [P, KT, SEQ], FP32R)
    an = late("an", [P, TT, HID])
    ah = late("ah", [P, KT, SEQ], FP32R)
    al = late("al", [P, KT, SEQ], FP32R)
    x1 = late("x1", [P, TT, HID])
    oy = late("oy", [P, SEQ])
    o_mask = late("o_mask", [P, SEQ], I32)
    o_alt = late("o_alt", [P, SEQ])
    sums = late("sums", [P, P])
    st2 = late("st2", [P, TT, 6])
    mv2 = late("mv2", [P, TT, 2])
    ve2 = late("ve2", [P, TT])
    rstd2 = late("rstd2", [P, TT])
    with ExitStack() as scope:
        sb = region(scope)
        sgn = sb("sgn", [P, IT, 3, HID], I8)
    with ExitStack() as scope:
        sb = region(scope)
        gate = sb("gate", [P, SEQ])
        hh = [sb(f"hh{p}", [P, SEQ], FP32R) for p in range(2)]
        hl = [sb(f"hl{p}", [P, SEQ], FP32R) for p in range(2)]
        res = sb("res", [P, TT, HID])

    psum = ctx.enter_context(nc.psum_tensor("psum", [P, 8, 512], FP32))
    BANK = [psum[:, i, :] for i in range(8)]

    x_in = sems("x_in", BATCH)
    w_in = sems("w_in", 3)
    scl_in = sem("scl_in")
    const_ok = sem("const_ok")
    wstat_ok = sem("wstat_ok")
    sgn_ok = sem("sgn_ok")
    sgnT_ok = sem("sgnT_ok")
    signs_ok = sem("signs_ok")
    fac_out = sem("fac_out")
    fac_in = sem("fac_in")
    stat_ch = sem("stat_ch")
    rstd_ok = sem("rstd_ok")
    dve_ch = sem("dve_ch")
    xn_ok = sems("xn_ok", 2)
    xT_ok = sems("xT_ok", 2)
    xh_ok = sems("xh_ok", 2)
    xl_ok = sems("xl_ok", 2)
    q_mm = sem("q_mm")
    yq_ok = sem("yq_ok")
    mask_ok = sem("mask_ok")
    yg_ok = sem("yg_ok")
    qh_ok = sem("qh_ok")
    ql_ok = sem("ql_ok")
    part_out = sems("part_out", 5)
    vT_mm = sem("vT_mm")
    v_ok = sem("v_ok")

    first_in = sems("first_in", 3)
    slot_in = sems("slot_in", 4)
    cleared = sem("cleared")
    slot_init = sem("slot_init")
    vs_ok = sem("vs_ok")
    s_mm = sem("s_mm")
    s_max = sem("s_max")
    mT_ok = sem("mT_ok")
    sh_hi = sem("sh_hi")
    sh_lo = sem("sh_lo")
    shift_in = sems("shift_in", 4)
    t_mm = sem("t_mm")
    exp_ok = sem("exp_ok")
    pv_mm = sem("pv_mm")
    u_ok = sem("u_ok")
    u_out = sems("u_out", 2)

    fw_in = sems("fw_in", 2)
    fd_ok = sem("fd_ok")
    fsgn_ok = sem("fsgn_ok")
    fsum_ok = sem("fsum_ok")

    sums_in = sem("sums_in")
    rec_out = sem("rec_out")
    an_in = sem("an_in")
    x_again = sem("x_again")
    rec_ok = sem("rec_ok")
    aT_ok = sem("aT_ok")
    ah_ok = sem("ah_ok")
    al_ok = sem("al_ok")
    o_mm = sem("o_mm")
    oy_ok = sem("oy_ok")
    x1_ok = sem("x1_ok")
    x1_out = sem("x1_out")
    c_ch = sem("c_ch")
    ve2_ok = sem("ve2_ok")
    rstd2_ok = sem("rstd2_ok")
    xn2_ok = sem("xn2_ok")
    x2T_mm = sem("x2T_mm")
    fxh_ok = sem("fxh_ok")
    fxl_ok = sem("fxl_ok")
    dtot_ok = sem("dtot_ok")
    ctot_mm = sem("ctot_mm")
    coeff_ok = sem("coeff_ok")
    m_in = sems("m_in", RING)
    w_ok = sem("w_ok")
    wT_mm = sem("wT_mm")
    wT_ok = sem("wT_ok")
    wh_ok = sem("wh_ok")
    wl_ok = sem("wl_ok")
    dh_ok = sem("dh_ok")
    dl_ok = sem("dl_ok")
    g_mm = sem("g_mm")
    u_mm = sem("u_mm")
    silu_ok = sem("silu_ok")
    h_ok = sem("h_ok")
    hh_ok = sem("hh_ok")
    hl_ok = sem("hl_ok")
    d_mm = sem("d_mm")
    res_in = sem("res_in")
    res_ok = sem("res_ok")
    out_done = sem("out_done")

    WEIGHT_SETS = ((QT, 4), (KTILE, 2), (OT, 4))
    LAST_G = GROUPS - 1
    GATE, UP, DOWN = 0, 1, 2
    NORM_STEP = KT + TT
    LAG = 4
    MT = KTILE + 2
    CREDIT = 4
    S_AHEAD = 14
    S_USES = GROUPS * 8

    SUMS_STEP = (0, 3)
    ATTENDED_STEP = (2, 0)
    SPLIT_STEP = (2, 1)
    MEANS_STEP = (2, 1)
    PROJECT_STEPS = [(2, 2), (2, 3), (3, 0), (3, 1)]
    NORM_TILES = (1, 2)
    MEAN_BANK = 0

    def att_bank(b, n):
        return n if isinstance(b, int) else 6 + n % 2

    def norm_bank(b, n):
        return (6, 7, 6, 7)[n] if isinstance(b, int) else (6, 7, GATE, UP)[n]

    block = ctx.enter_context(nc.Block())

    def load_group(eng, g, s, done):
        for copy in range(2):
            eng.dma_start(q_slot[s][32 * copy:32 * copy + 32].bitcast(FP32),
                         q_dram[bass.ds(g, 1)].rearrange("o l d j t -> (o l d) j t")
                         ).then_inc(done, 16)
        eng.dma_start(k_slot[s][0:SHIFT_ROW].bitcast(FP32),
                     k_dram[bass.ds(g, 1)].rearrange("o r t -> (o r) t")).then_inc(done, 16)

    @block.sync
    def _(sp):
        for b in range(BATCH):
            sp.dma_start(x_sb[:, b * TT:(b + 1) * TT, :],
                         x[b].rearrange("(t p) c -> p t c", p=P)).then_inc(x_in[b], 16)
        for m in range(5):
            sp.nop(nofuse=True).then_inc(part_out[m], 64)
        for s in range(3):
            sp.nop(nofuse=True).then_inc(slot_in[s], 48)
        sp.wait_ge(wstat_ok, 5)
        sp.dma_start(fac_dram.rearrange("a w p -> p a w"), wstat[:, 3:5, :],
                     allow_slow_non_contiguous=True).then_inc(fac_out, 16)
        sp.wait_ge(fac_out, 16)
        sp.dma_start(fac_row[:].rearrange("p a t c -> p a (t c)"),
                     fac_dram[:, OT:].rearrange("a w p -> a (w p)").unsqueeze(0).to_broadcast([P, 2, KT * P])
                     ).then_inc(fac_in, 16)

        with sp.Fori(0, 2) as i:
            for p in range(2):
                b = 2 * i + p
                for m in range(5):
                    for part, (src, ready) in enumerate(((q_hi, qh_ok), (q_lo, ql_ok))):
                        sp.wait_ge(ready, (0, CREDIT)[part] + 5 * b + m + 1)
                        if m < 4:
                            for half_tile in range(2):
                                g = 8 * b + 2 * m + half_tile
                                dst = q_dram[bass.ds(g, 1), part].rearrange("o d j t -> (o j) d t")
                                rows = src[64 * half_tile:64 * half_tile + 64, m, :].bitcast(FP32)
                                sp.dma_start(dst, rows).then_inc(part_out[m], 16)
                        else:
                            for copy in range(2):
                                r = (2 * part + copy) * HEAD_DIM
                                dst = k_dram[bass.ds(8 * b, 8), r:r + HEAD_DIM, :]
                                sp.dma_start(dst, src[:, m, :].bitcast(FP32)).then_inc(part_out[m], 16)

        def load_shift(g, s):
            for part, ready in enumerate((sh_hi, sh_lo)):
                sp.wait_ge(ready, g + 1)
                sp.dma_start(q_slot[s][SHIFT_ROW + part:SHIFT_ROW + part + 1].bitcast(FP32).rearrange("o j (t c) -> o (j t) c", c=P),
                             shift[s % 2][:, part, :].bitcast(FP32)).then_inc(shift_in[s], 16)

        def store_values(g, s):
            sp.wait_ge(u_ok, g + 1)
            sp.dma_start(u_dram.rearrange("b k r c t -> (b k r c) t")[bass.ds(P * g, P)], u_sb[s % 2][:]
                         ).then_inc(u_out[s % 2], 16)

        sp.wait_ge(v_ok, BATCH)
        for m in range(5):
            sp.wait_ge(part_out[m], (BATCH + 1) * 64)
        sp.wait_ge(slot_init, 14)
        load_shift(0, 0)

        def load_tile(e, dst, sources, done):
            for k in range(2):
                sp.dma_start(dst[:, k, :], sources[k][bass.ds(e * P, P), :]).then_inc(done, 16)
            sp.dma_start(dst[:, 2, :].rearrange("p (t c) -> p t c", c=P),
                         sources[2][:, bass.ds(e * P, P)].rearrange("(t p) c -> p t c", p=P)).then_inc(done, 16)

        def load_sums(b):
            settle(sp)
            for k in range(KT):
                sp.dma_start(sums[2 * REP * TT * k:2 * REP * TT * (k + 1)],
                             u_dram[bass.ds(b, 1), k, :, HEAD_DIM, :].rearrange("o r (q t) -> (o r) q t", q=TT)
                             ).then_inc(sums_in, 16)

        def load_batch(b):
            sp.dma_start(x1[:], x[bass.ds(b, 1)].rearrange("o (t p) c -> (o p) t c", p=P)).then_inc(x_again, 16)
            for kt in range(KT):
                sp.dma_start(an[:, kt, :], u_dram[bass.ds(b, 1), kt].rearrange("o r c t -> (o r) c t")[:, 0:HEAD_DIM, :]
                             ).then_inc(an_in, 16)

        def load_reciprocals(b):
            sp.wait_ge(rec_ok, b + 1)
            settle(sp)
            sp.dma_start(rec_dram[bass.ds(b, 1)].rearrange("o h (q t) -> (o h q) t", q=TT), sums[:]).then_inc(rec_out, 16)
            sp.wait_ge(rec_out, 16 * (b + 1))
            settle(sp)
            for kt in range(KT):
                heads = rec_dram[bass.ds(b, 1), 2 * REP * kt:2 * REP * (kt + 1), :].rearrange("o h t -> (o h) t")
                sp.dma_start(al[:, kt, :].bitcast(FP32), heads.unsqueeze(1).to_broadcast([2 * REP, HEAD_DIM, SEQ])
                             ).then_inc(an_in, 16)

        def sp_steps(i, first=False, last=False):
            for s in range(4):
                g = 4 * i + s
                if s % 2 == 0 and not last:
                    h = s // 2
                    if not first:
                        sp.wait_ge(fsum_ok, 3 * (2 * i + h - 1))
                        sp.wait_ge(fsgn_ok, 3 * (2 * i + h - 1))
                        settle(sp)
                    load_tile(2 * i + h, wn[h], (w1, w3, w2), fw_in[h])
                    load_tile(2 * i + h, mn[h], (m1, m3, m2), fw_in[h])
                if not (last and s > 0):
                    positive(sp, t_mm, 16 * g)
                    load_group(sp, g + 3, (s + 3) % 4, slot_in[(s + 3) % 4])
                if not (last and s == 3):
                    load_shift(g + 1, (s + 1) % 4)
                if last and s == 0:
                    for p in range(2):
                        sp.wait_ge(u_out[p], 16 * KV_HEADS // 2)
                    load_sums(0)
                    load_batch(0)
                if last and s == 1:
                    load_reciprocals(0)
                if last and s >= 2:
                    if s == 2:
                        sp.wait_ge(fsum_ok, 3 * IT)
                        sp.wait_ge(fsgn_ok, 3 * IT)
                    for e in range(2 * (s - 2), 2 * (s - 1)):
                        load_tile(e, stage[e], (m1, m3, m2), m_in[e])
                if not (first and s == 0):
                    store_values(g - 1, s + 3)

        sp_steps(0, first=True)
        with sp.Fori(1, GROUPS // 4 - 1) as i:
            sp_steps(i)
        sp_steps(GROUPS // 4 - 1, last=True)
        store_values(LAST_G, 3)

        def store_residual(b):
            sp.wait_ge(x1_ok, 4 * (b + 1))
            settle(sp)
            sp.dma_start(x1_dram[bass.ds(4 * b, 4)].rearrange("t p c -> p t c"), x1[:]).then_inc(x1_out, 16)

        for e in range(RING, IT):
            sp.wait_ge(wT_mm, 3 * (e - RING + 1))
            load_tile(e, stage[e % RING], (m1, m3, m2), m_in[e % RING])
        store_residual(0)
        for p in range(2):
            sp.wait_ge(u_out[p], 16 * GROUPS // 2)

        def finish_batch(b):
            settle(sp)
            sp.wait_ge(x1_out, 16 * (b + 1))
            settle(sp)
            sp.dma_start(res[:], x1_dram[bass.ds(4 * b, TT)].rearrange("t p c -> p t c")).then_inc(res_in, 16)
            for t in range(TT):
                sp.wait_ge(res_ok, CREDIT + 4 * b + t + 1)
                settle(sp)
                sp.dma_start(out[bass.ds(b, 1), t * P:(t + 1) * P, :].rearrange("o p c -> (o p) c"),
                             res[:, t, :]).then_inc(out_done, 16)

        sp.wait_ge(wT_mm, 3 * IT)
        with sp.Fori(0, BATCH - 1) as b:
            load_sums(b + 1)
            sp.wait_ge(x2T_mm, 4 * (b + 1))
            settle(sp)
            sp.wait_ge(x1_out, 16 * (b + 1))
            settle(sp)
            sp.wait_ge(xn2_ok, 4 * (b + 1))
            settle(sp)
            sp.wait_ge(o_mm, 4 * (b + 1))
            settle(sp)
            load_batch(b + 1)
            load_reciprocals(b + 1)
            store_residual(b + 1)
            finish_batch(b)
            sp.wait_ge(out_done, 64 * (b + 1))
            settle(sp)
        finish_batch(BATCH - 1)
        sp.wait_ge(out_done, 64 * BATCH)


    @block.gpsimd
    def _(pool):
        nc.gpsimd.memset(ident[:], 0.0).then_inc(const_ok, 1)
        pool.wait_ge(const_ok, 1)
        nc.gpsimd.affine_select(out=ident[:], in_=ident[:], compare_op=ALU.not_equal, fill=1.0, base=0,
                                pattern=[[-1, P]], channel_multiplier=1).then_inc(const_ok, 1)
        pool.wait_ge(const_ok, 2)
        nc.gpsimd.tensor_copy(ident16[:], ident[:]).then_inc(const_ok, 1)
        nc.gpsimd.memset(half[:], -0.5).then_inc(const_ok, 1)
        nc.gpsimd.memset(ones[:], 1.0).then_inc(const_ok, 1)
        pool.wait_ge(const_ok, 5)
        pool.wait_ge(stat_ch, 2 * NT + 1)
        nc.gpsimd.tensor_tensor(rstd[:], ve[:], half[:], ALU.pow).then_inc(rstd_ok, 1)

        pool.wait_ge(sgnT_ok, WTILES)
        pool.wait_ge(rstd_ok, 1)
        for s in range(4):
            nc.gpsimd.memset(k_slot[s][SHIFT_ROW:STACK].bitcast(FP32), 0.0).then_inc(slot_init, 1)
        pool.wait_ge(slot_init, 4)
        for s in range(2):
            nc.gpsimd.memset(v_slot[s][:, :, HEAD_DIM:], 1.0).then_inc(slot_init, 1)
        pool.wait_ge(slot_init, 6)
        for s in range(4):
            nc.gpsimd.memset(k_slot[s][SHIFT_ROW:SHIFT_ROW + 2].bitcast(FP32), 1.0).then_inc(slot_init, 1)
        pool.wait_ge(slot_init, 10)
        for p in range(2):
            pool.wait_ge(xn_ok[p], 8)
        for s in range(4):
            nc.gpsimd.memset(q_slot[s][SHIFT_ROW:STACK].bitcast(FP32), 0.0).then_inc(slot_init, 1)

        for m in range(5):
            pool.wait_ge(part_out[m], 2 * 64)
        for g in range(3):
            load_group(nc.gpsimd, g, g, first_in[g])

        def clear_shift(g, s):
            settle(pool)
            nc.gpsimd.memset(q_slot[s][SHIFT_ROW:SHIFT_ROW + 2].bitcast(FP32), 0.0).then_inc(cleared, 1)

        def fill_values(g, s):
            settle(pool)
            nc.gpsimd.tensor_copy(v_slot[s][:, :, 0:HEAD_DIM],
                                  v_sb[:, bass.ds(g, 1), :, :].rearrange("p o t d -> p (o t) d")).then_inc(vs_ok, 1)

        pool.wait_ge(slot_init, 14)
        pool.wait_ge(v_ok, BATCH)
        fill_values(0, 0)
        fill_values(1, 1)

        def pool_steps(i, first=False, last=False):
            for s in range(4):
                g = 4 * i + s
                if s % 2 == 1 and not last:
                    h = s // 2
                    pool.wait_ge(vs_ok, g + 1)
                    settle(pool)
                    pool.wait_ge(fw_in[h], 96 * (i + 1))
                    nc.gpsimd.tensor_tensor(wn[h][:], wn[h][:], mn[h][:], ALU.subtract).then_inc(fd_ok, 1)
                    pool.wait_ge(fd_ok, 2 * i + h + 1)
                if not (first and s == 0):
                    if not (last and s > 0):
                        pool.wait_ge(t_mm, 16 * g)
                        pool.wait_ge(vs_ok, g + 1)
                        clear_shift(g + 3, (s + 3) % 4)
                    if not (last and s == 3):
                        pool.wait_ge(pv_mm, 4 * g)
                        if not (last and s > 0):
                            pool.wait_ge(cleared, g)
                        fill_values(g + 1, (s + 1) % 2)

        pool_steps(0, first=True)
        with pool.Fori(1, GROUPS // 4 - 1) as i:
            pool_steps(i)
        pool_steps(GROUPS // 4 - 1, last=True)

        def norm_factor(b):
            pool.wait_ge(ve2_ok, b + 1)
            nc.gpsimd.tensor_tensor(rstd2[:], ve2[:], half[:, 0:TT], ALU.pow).then_inc(rstd2_ok, 1)

        norm_factor(0)
        def split_down(b, e, src, parity):
            n = IT * b + e
            pool.wait_ge(d_mm, CREDIT + n - 1)
            settle(pool)
            nc.gpsimd.tensor_copy(dh[parity][:], w2T[:, bass.ds(src, 1), :].rearrange("p o c -> p (o c)")
                                  ).then_inc(dh_ok, 1)

        pool.wait_ge(wT_ok, 3 * IT)
        with pool.Fori(0, BATCH - 1) as b:
            for e in range(LAG + NORM_STEP + 1):
                split_down(b, e, e, e % 2)
            norm_factor(b + 1)
            for e in range(LAG + NORM_STEP + 1, IT):
                split_down(b, e, e, e % 2)
        with pool.Fori(0, IT // 2) as i:
            for p in range(2):
                split_down(BATCH - 1, 2 * i + p, 2 * i + p, p)

    @block.scalar
    def _(act):
        act.nop(nofuse=True).then_inc(silu_ok, CREDIT)
        act.nop(nofuse=True).then_inc(yq_ok, CREDIT)
        def load_weight(src, t0, tiles, done):
            act.dma_start(w_nat[:, t0:t0 + tiles, :], src.rearrange("(t p) c -> p t c", p=P)).then_inc(done, 16)

        load_weight(q_w, QT, 4, w_in[0])
        load_weight(k_w, KTILE, 1, w_in[1])
        load_weight(v_w, VTILE, 1, w_in[1])
        load_weight(o_w, OT, 4, w_in[2])
        for src, t0, tiles in ((q_s, QT, 4), (k_s, KTILE, 1), (v_s, VTILE, 1), (o_s, OT, 4)):
            act.dma_start(scl[:, t0:t0 + tiles], src.rearrange("(t p) -> p t", p=P),
                          allow_slow_non_contiguous=True).then_inc(scl_in, 16)
        for n, (t0, tiles) in enumerate(WEIGHT_SETS):
            act.wait_ge(wstat_ok, n + 1)
            for m in range(t0, t0 + tiles):
                nc.scalar.activation(w_sgn[:, m, :], w_nat[:, m, :], ACT.Sign,
                                     scale=wstat[:, 2, m:m + 1]).then_inc(sgn_ok, 1)
            for m in range(t0, t0 + tiles):
                act.wait_ge(sgnT_ok, m + 1)
                dst = signs[:, :, m * P:(m + 1) * P] if m < OT else signs_o[:, :, (m - OT) * P:(m - OT + 1) * P]
                src = BANK[m % 4].bitcast(BF16)[:, 0:HID].rearrange("p (t c) -> p t c", c=P)
                nc.scalar.activation(dst, src, ACT.Copy).then_inc(signs_ok, 1)
        act.wait_ge(wstat_ok, 5)

        def scale_tile(b, m, slot):
            n = MT * b + m
            act.wait_ge(q_mm, n + 1)
            act.wait_ge(yg_ok, CREDIT + n + 1 - Y_RING)
            nc.scalar.activation(yq[slot], BANK[4 + m % 3], ACT.Copy, scale=wstat[:, 3, m:m + 1]).then_inc(yq_ok, 1)

        def hi_tile(b, m):
            act.wait_ge(yg_ok, CREDIT + MT * b + m + 1)
            act.wait_ge(part_out[m], 64 * (b + 1))
            nc.scalar.activation(q_hi[:, m, :], g_alt[m % 2][:], ACT.Copy).then_inc(qh_ok, 1)

        def values_out(b):
            act.wait_ge(vT_mm, CREDIT + b + 1)
            nc.scalar.activation(v_sb[:, bass.ds(KV_HEADS * b, KV_HEADS), :, :],
                                 BANK[7].rearrange("p (t h d) -> p h t d", t=TT, d=HEAD_DIM), ACT.Copy).then_inc(v_ok, 1)

        with act.Fori(0, 2) as i:
            for p in range(2):
                for kt in range(KT):
                    act.wait_ge(xT_ok[p], CREDIT + 4 * i + kt + 1)
                    nc.scalar.activation(xh[p][:, kt, :], BANK[kt], ACT.Copy).then_inc(xh_ok[p], 1)
            for p in range(2):
                b = 2 * i + p
                for m in range(MT):
                    scale_tile(b, m, (MT * p + m) % Y_RING)
                    if m > 0:
                        hi_tile(b, m - 1)
                    if p == 1 and m == 1:
                        values_out(b - 1)
            values_out(2 * i + 1)

        act.wait_ge(v_ok, BATCH)

        def hi_attended(b, kt):
            act.wait_ge(aT_ok, 4 * b + kt + 1)
            positive(act, o_mm, 4 * b)
            nc.scalar.activation(ah[:, kt, :], an[:, kt, :], ACT.Copy).then_inc(ah_ok, 1)

        def hi_norm(b, kt):
            act.wait_ge(x2T_mm, 4 * b + kt + 1)
            positive(act, u_mm, IT * b)
            nc.scalar.activation(fxh[:, kt, :], BANK[norm_bank(b, kt)], ACT.Copy).then_inc(fxh_ok, 1)

        def act_steps(i, first=False, last=False):
            base = 4 * i
            for s in range(4):
                g = base + s
                for kt in range(TT):
                    for j in range(REP):
                        act.wait_ge(t_mm, 16 * g + 4 * kt + j + 1)
                        if j == 0:
                            positive(act, pv_mm, 4 * g + kt - 3)
                        nc.scalar.activation(probs[kt][:, j, :], BANK[4 + j % 2], ACT.Exp,
                                             scale=HEAD_DIM ** -0.5).then_inc(exp_ok, 1)
                        if kt == 0 and j == REP - 1 and not (first and s == 0):
                            reused = None if first and s < 3 else 4 * 2 * base + 16 * ((s - 3) // 2 + 1)
                            copy_u(g - 1, s - 1, reused)
                    if last and (s, kt) == SPLIT_STEP:
                        for k in range(KT):
                            hi_attended(0, k)
                    if s % 2 == 1 and kt > 0 and not last:
                        e = 2 * i + s // 2
                        act.wait_ge(fd_ok, e + 1)
                        nc.scalar.activation(sgn[:, bass.ds(e, 1), kt - 1, :].rearrange("p o c -> p (o c)"),
                                             wn[s // 2][:, kt - 1, :], ACT.Sign).then_inc(fsgn_ok, 1)

        def copy_u(g, s, reused):
            act.wait_ge(pv_mm, 4 * g + 4)
            if reused is not None:
                act.wait_ge(u_out[s % 2], reused)
            nc.scalar.activation(u_sb[s % 2][:], BANK[6], ACT.Copy).then_inc(u_ok, 1)

        act_steps(0, first=True)
        with act.Fori(1, GROUPS // 4 - 1) as i:
            act_steps(i)
        act_steps(GROUPS // 4 - 1, last=True)
        copy_u(LAST_G, 3, 16 * (GROUPS // 2 - 1))

        def weights_out(e):
            for k, dst in enumerate((w1T, w3T, w2T)):
                act.wait_ge(wT_mm, 3 * e + k + 1)
                nc.scalar.activation(dst[:, e, :], BANK[3 * (e % 2) + k], ACT.Copy).then_inc(wT_ok, 1)

        for p in range(2):
            act.wait_ge(u_out[p], 16 * GROUPS // 2)
        for e in range(IT - 1):
            weights_out(e)
            if e + 1 in NORM_TILES:
                n = 2 * NORM_TILES.index(e + 1)
                hi_norm(0, n)
                hi_norm(0, n + 1)
        weights_out(IT - 1)
        def hi_gate_up(n, src, parity):
            if n is not None:
                act.wait_ge(u_mm, n - 1)
            for k, w in enumerate((w1T, w3T)):
                nc.scalar.activation(wh[parity][:, k, :], w[:, bass.ds(src, 1), :].rearrange("p o c -> p (o c)"),
                                     ACT.Copy).then_inc(wh_ok, 1)

        def act_tile(b, e, nxt, p):
            n = IT * b + e
            act.wait_ge(g_mm, n + 1)
            act.wait_ge(hl_ok, CREDIT + n)
            nc.scalar.activation(gate[:], BANK[GATE], ACT.Silu).then_inc(silu_ok, 1)
            act.wait_ge(h_ok, CREDIT + n + 1)
            act.wait_ge(d_mm, CREDIT + n - 1)
            nc.scalar.activation(hh[p][:], gate[:], ACT.Copy).then_inc(hh_ok, 1)
            if nxt is not None:
                hi_gate_up(n + 2, nxt, p)

        act.wait_ge(wT_ok, 3 * IT)
        for p in range(2):
            hi_gate_up(None, p, p)
        with act.Fori(0, BATCH - 1) as b:
            for e in range(IT):
                act_tile(b, e, (e + 2) % IT, e % 2)
                if LAG <= e < LAG + KT:
                    hi_attended(b + 1, e - LAG)
            for kt in range(KT):
                hi_norm(b + 1, kt)
        with act.Fori(0, IT // 2 - 1) as i:
            for p in range(2):
                act_tile(BATCH - 1, 2 * i + p, 2 * i + p + 2, p)
        for e in range(IT - 2, IT):
            act_tile(BATCH - 1, e, None, e % 2)

    @block.vector
    def _(dve):
        dve.nop(nofuse=True).then_inc(h_ok, CREDIT)
        dve.nop(nofuse=True).then_inc(yg_ok, CREDIT)
        dve.nop(nofuse=True).then_inc(ql_ok, CREDIT)
        dve.nop(nofuse=True).then_inc(xl_ok[0], CREDIT)
        dve.nop(nofuse=True).then_inc(xl_ok[1], CREDIT)
        dve.nop(nofuse=True).then_inc(hl_ok, CREDIT)
        dve.nop(nofuse=True).then_inc(res_ok, CREDIT)
        v = nc.vector
        chain = Chain(dve, dve_ch)

        def token_stats(b):
            dve.wait_ge(x_in[b], 16)
            for t in range(TT * b, TT * (b + 1)):
                v.bn_stats(stats[:, t, :], x_sb[:, t, :]).then_inc(stat_ch, 1)

        def weight_scales(n):
            t0, tiles = WEIGHT_SETS[n]
            c = slice(t0, t0 + tiles)
            dve.wait_ge(w_in[n], (16, 32, 16)[n])
            chain.link(v.tensor_reduce(wstat[:, 0, c], w_nat[:, c, :], AX.X, ALU.add, apply_absolute_value=True))
            chain.link(v.tensor_scalar(wstat[:, 1, c], wstat[:, 0, c], 1.0 / HID, 1e-8, ALU.mult, ALU.max))
            v.reciprocal(wstat[:, 2, c], wstat[:, 1, c]).then_inc(wstat_ok, 1)

        token_stats(0)
        weight_scales(0)
        token_stats(1)
        weight_scales(1)
        token_stats(2)
        token_stats(3)
        dve.wait_ge(stat_ch, NT)
        for t in range(NT):
            v.bn_aggr(mv[:, t, :], stats[:, t, :]).then_inc(stat_ch, 1)
        dve.wait_ge(stat_ch, 2 * NT)
        v.tensor_scalar(ve[:], mv[:, :, 1], EPS, None, ALU.add).then_inc(stat_ch, 1)
        weight_scales(2)
        dve.wait_ge(scl_in, 64)
        chain.link(v.tensor_tensor(wstat[:, 5, :], wstat[:, 1, :], scl[:], ALU.mult))
        v.tensor_scalar(wstat[:, 3, :], wstat[:, 5, :], -FLT_MAX, FLT_MAX, ALU.max, ALU.min).then_inc(wstat_ok, 1)
        chain.link(v.tensor_scalar(wstat[:, 0, :], wstat[:, 5, :], 0.0, 0.0, ALU.mult, ALU.is_equal))
        v.tensor_scalar(wstat[:, 4, :], wstat[:, 0, :], -1.0, 1.0, ALU.mult, ALU.add).then_inc(wstat_ok, 1)
        dve.wait_ge(wstat_ok, 5)
        dve.wait_ge(rstd_ok, 1)

        def norm(i, p):
            for t in range(TT):
                tile = 4 * (2 * i + p) + t
                dve.wait_ge(xT_ok[p], CREDIT + 4 * i)
                v.tensor_scalar(xn[p][:, t, :], x_sb[:, bass.ds(tile, 1), :].rearrange("p o c -> p (o c)"),
                                mv[:, bass.ds(tile, 1), 0:1].rearrange("p o c -> p (o c)"),
                                rstd[:, bass.ds(tile, 1)], ALU.subtract, ALU.mult).then_inc(xn_ok[p], 1)

        def guard(b, m, slot):
            y, alt, mask = yq[slot], g_alt[m % 2][:], g_mask[m % 2][:]
            dve.wait_ge(yq_ok, CREDIT + MT * b + m + 1)
            if m == 1:
                dve.wait_ge(vT_mm, CREDIT + b)
            else:
                dve.wait_ge(ql_ok, CREDIT + 5 * b + max(m - 1, 0))
            v.tensor_scalar(alt, y, GUARD, -GUARD, ALU.min, ALU.max)
            v.tensor_scalar(mask, y, wstat[:, 4, m:m + 1], 0.0, ALU.mult, ALU.is_equal).then_inc(mask_ok, 1)
            if m > 0:
                lo_tile(b, m - 1)
            dve.wait_ge(mask_ok, MT * b + m + 1)
            settle(dve)
            v.copy_predicated(alt, mask, y).then_inc(yg_ok, 1)

        def lo_tile(b, m):
            dve.wait_ge(qh_ok, 5 * b + m + 1)
            v.tensor_tensor(q_lo[:, m, :], g_alt[m % 2][:], q_hi[:, m, :].bitcast(FP32), ALU.subtract).then_inc(ql_ok, 1)

        with dve.Fori(0, 2) as i:
            for p in range(2):
                norm(i, p)
            for p in range(2):
                for kt in range(KT):
                    dve.wait_ge(xh_ok[p], 4 * i + kt + 1)
                    v.tensor_tensor(xl[p][:, kt, :], BANK[kt], xh[p][:, kt, :].bitcast(FP32),
                                    ALU.subtract).then_inc(xl_ok[p], 1)
            for p in range(2):
                for m in range(MT):
                    guard(2 * i + p, m, (MT * p + m) % Y_RING)

        def maxima(base, nn):
            rel, j, half_tile = nn // 8, nn % 8 // 2, nn % 2
            c = j * TT + 2 * half_tile
            dve.wait_ge(s_mm, 8 * base + nn + 1)
            pair = psum[:, 2 * half_tile:2 * half_tile + 2, :]
            v.tensor_reduce(nmx[rel % 2][:, c:c + 2], pair, AX.X, ALU.max, negate=True).then_inc(s_max, 1)

        def split_shift(g, s, reused):
            dve.wait_ge(mT_ok, g + 1)
            if reused is not None:
                dve.wait_ge(shift_in[(s + 2) % 4], reused)
            src = BANK[7][0:REP * TT, 0:P]
            v.tensor_scalar(shift[s % 2][:, 0, :], src, -SHIFT_MAX, SHIFT_MAX, ALU.max, ALU.min).then_inc(sh_hi, 1)
            dve.wait_ge(sh_hi, g + 1)
            v.scalar_tensor_tensor(shift[s % 2][:, 1, :], src, -SHIFT_MAX, shift[s % 2][:, 0, :].bitcast(FP32),
                                   ALU.max, ALU.subtract).then_inc(sh_lo, 1)

        def invert_sums(b):
            dve.wait_ge(sums_in, 64 * (b + 1))
            v.reciprocal(sums[:], sums[:]).then_inc(rec_ok, 1)

        def attended(b, kt):
            if kt == 0:
                dve.wait_ge(an_in, 128 * (b + 1))
            v.tensor_tensor(an[:, kt, :], an[:, kt, :], al[:, kt, :].bitcast(FP32), ALU.mult).then_inc(aT_ok, 1)

        def lo_attended(b, kt):
            dve.wait_ge(ah_ok, 4 * b + kt + 1)
            v.tensor_tensor(al[:, kt, :], an[:, kt, :], ah[:, kt, :].bitcast(FP32), ALU.subtract).then_inc(al_ok, 1)

        def lo_norm(b, kt):
            dve.wait_ge(fxh_ok, 4 * b + kt + 1)
            v.tensor_tensor(fxl[:, kt, :], BANK[norm_bank(b, kt)], fxh[:, kt, :].bitcast(FP32), ALU.subtract
                            ).then_inc(fxl_ok, 1)

        def residual(b, t, chain):
            row = [fac_row[:, a, :, :].rearrange("p t c -> p (t c)") for a in range(2)]
            y = oy[:]
            dve.wait_ge(o_mm, 4 * b + t + 1)
            v.tensor_tensor(y, BANK[att_bank(b, t)], row[0], ALU.mult).then_inc(oy_ok, 1)
            dve.wait_ge(oy_ok, 4 * b + t + 1)
            chain.link(v.tensor_tensor(o_alt[:], y, y, ALU.is_equal))
            chain.link(v.scalar_tensor_tensor(o_alt[:], o_alt[:], GUARD, y, ALU.mult, ALU.min))
            v.tensor_scalar(o_alt[:], o_alt[:], -GUARD, None, ALU.max)
            chain.link(v.scalar_tensor_tensor(o_mask[:], y, 0.0, row[1], ALU.mult, ALU.is_equal))
            settle(dve)
            chain.link(v.copy_predicated(o_alt[:], o_mask[:], y))
            if t == 0:
                dve.wait_ge(x_again, 16 * (b + 1))
            v.tensor_tensor(x1[:, t, :], x1[:, t, :], o_alt[:], ALU.add).then_inc(x1_ok, 1)
            dve.wait_ge(x1_ok, 4 * b + t + 1)
            chain.link(v.bn_stats(st2[:, t, :], x1[:, t, :]))

        def second_norm(b, chain):
            settle(dve)
            for t in range(TT):
                last = v.bn_aggr(mv2[:, t, :], st2[:, t, :])
            chain.link(last)
            v.tensor_scalar(ve2[:], mv2[:, :, 1], EPS, None, ALU.add).then_inc(ve2_ok, 1)
            dve.wait_ge(rstd2_ok, b + 1)
            dve.wait_ge(al_ok, 4 * (b + 1))
            for t in range(TT):
                v.tensor_scalar(an[:, t, :], x1[:, t, :], mv2[:, t, 0:1], rstd2[:, t:t + 1],
                                ALU.subtract, ALU.mult).then_inc(xn2_ok, 1)

        per_batch = TT * 5 + 1
        c_chain = Chain(dve, c_ch)

        def weight_means():
            dve.wait_ge(fac_in, 16)
            dve.wait_ge(fsum_ok, 3 * IT)
            v.tensor_reduce(dtot[:], dsum[:], AX.X, ALU.add).then_inc(dtot_ok, 1)
            dve.wait_ge(ctot_mm, 1)
            v.tensor_scalar(coeff[:], BANK[MEAN_BANK][:, 0:3], 1.0 / (INTER * HID), None, ALU.mult).then_inc(coeff_ok, 1)

        def dve_steps(i, first=False, last=False):
            base = 4 * i
            for s in range(4):
                g = base + s
                for kt in range(TT):
                    for a in range(2):
                        nn = 8 * s + 2 * kt + a + S_AHEAD
                        if not (last and nn >= 32):
                            maxima(base, nn)
                        if s % 2 == 1 and kt != 2 and a == 1 and not last:
                            k = min(kt, 2)
                            dve.wait_ge(fd_ok, 2 * i + s // 2 + 1)
                            v.tensor_reduce(dsum[:, k, bass.ds(2 * i + s // 2, 1)], wn[s // 2][:, k, :], AX.X, ALU.add,
                                            apply_absolute_value=True).then_inc(fsum_ok, 1)
                        if kt == 1 and a == 1 and not (last and s == 3):
                            n = s + 1
                            reused = None if first and s == 0 else 32 * i + (32 if n >= 2 else 0)
                            split_shift(g + 1, n % 4, reused)
                    if last and (s, kt) == SUMS_STEP:
                        invert_sums(0)
                    if last and (s, kt) == MEANS_STEP:
                        weight_means()
                    if last and (s, kt) == ATTENDED_STEP:
                        for k in range(KT):
                            attended(0, k)
                    if last and (s, kt) == SPLIT_STEP:
                        for k in range(KT):
                            lo_attended(0, k)
                    if last and (s, kt) in PROJECT_STEPS:
                        residual(0, PROJECT_STEPS.index((s, kt)), c_chain)

        for nn in range(S_AHEAD):
            maxima(0, nn)
            if nn == 8:
                split_shift(0, 0, None)
        dve_steps(0, first=True)
        with dve.Fori(1, GROUPS // 4 - 1) as i:
            dve_steps(i)
        dve_steps(GROUPS // 4 - 1, last=True)
        second_norm(0, c_chain)
        dve.wait_ge(coeff_ok, 1)
        dve.wait_ge(fsgn_ok, 3 * IT)
        for e in range(IT):
            slot = e % RING
            dve.wait_ge(m_in[slot], 48 * (e // RING + 1))
            for k in range(3):
                v.scalar_tensor_tensor(stage[slot][:, k, :], sgn[:, e, k, :], coeff[:, k:k + 1], stage[slot][:, k, :],
                                       ALU.mult, ALU.add).then_inc(w_ok, 1)
            if e in NORM_TILES:
                n = 2 * NORM_TILES.index(e)
                lo_norm(0, n)
                lo_norm(0, n + 1)

        def lo_gate_up(done, src, parity):
            for k, w in enumerate((w1T, w3T)):
                dve.wait_ge(wh_ok, done + k + 1)
                v.tensor_tensor(wl[parity][:, k, :], w[:, bass.ds(src, 1), :].rearrange("p o c -> p (o c)"),
                                wh[parity][:, k, :].bitcast(FP32), ALU.subtract).then_inc(wl_ok, 1)

        def dve_tile(b, e, src, nxt, p):
            n = IT * b + e
            dve.wait_ge(silu_ok, CREDIT + n + 1)
            dve.wait_ge(u_mm, n + 1)
            v.tensor_tensor(gate[:], gate[:], BANK[UP], ALU.mult).then_inc(h_ok, 1)
            dve.wait_ge(hh_ok, n + 1)
            v.tensor_tensor(hl[p][:], gate[:], hh[p][:].bitcast(FP32), ALU.subtract).then_inc(hl_ok, 1)
            dve.wait_ge(dh_ok, n + 1)
            v.tensor_tensor(dl[p][:], w2T[:, bass.ds(src, 1), :].rearrange("p o c -> p (o c)"),
                            dh[p][:].bitcast(FP32), ALU.subtract).then_inc(dl_ok, 1)
            if nxt is not None:
                lo_gate_up(2 * (n + 2), nxt, p)

        def results(b):
            dve.wait_ge(d_mm, CREDIT + IT * (b + 1))
            dve.wait_ge(res_in, 16 * (b + 1))
            for t in range(TT):
                v.tensor_tensor(res[:, t, :], BANK[DOWN + t], res[:, t, :], ALU.add).then_inc(res_ok, 1)

        for p in range(2):
            lo_gate_up(2 * p, p, p)
        with dve.Fori(0, BATCH - 1) as b:
            c_chain.enter(b, per_batch)
            for e in range(IT):
                dve_tile(b, e, e, (e + 2) % IT, e % 2)
                if e == 0:
                    invert_sums(b + 1)
                if LAG <= e < LAG + KT:
                    lo_attended(b + 1, e - LAG)
                if LAG <= e + 1 < LAG + KT:
                    attended(b + 1, e + 1 - LAG)
                if LAG + KT <= e < LAG + KT + TT:
                    residual(b + 1, e - LAG - KT, c_chain)
                elif e == LAG + NORM_STEP:
                    second_norm(b + 1, c_chain)
            for kt in range(KT):
                lo_norm(b + 1, kt)
            results(b)
            c_chain.leave(BATCH - 1)
        with dve.Fori(0, IT // 2 - 1) as i:
            for p in range(2):
                dve_tile(BATCH - 1, 2 * i + p, 2 * i + p, 2 * i + p + 2, p)
        for e in range(IT - 2, IT):
            dve_tile(BATCH - 1, e, e, None, e % 2)
        results(BATCH - 1)

    @block.tensor
    def _(pe):
        pe.nop(nofuse=True).then_inc(d_mm, CREDIT)
        pe.nop(nofuse=True).then_inc(vT_mm, CREDIT)
        pe.nop(nofuse=True).then_inc(xT_ok[0], CREDIT)
        pe.nop(nofuse=True).then_inc(xT_ok[1], CREDIT)
        mm, tr = nc.tensor.matmul, nc.tensor.transpose
        pe.wait_ge(const_ok, 5)
        for m in range(WTILES):
            pe.wait_ge(sgn_ok, m + 1)
            positive(pe, signs_ok, m - 3)
            for kt in range(KT):
                last = tr(BANK[m % 4].bitcast(BF16)[:, kt * P:(kt + 1) * P], w_sgn[:, m, kt * P:(kt + 1) * P], ident16[:])
            last.then_inc(sgnT_ok, 1)
        pe.wait_ge(signs_ok, WTILES)

        def transpose_values_in(b):
            pe.wait_ge(yg_ok, CREDIT + MT * (b + 1))
            for t in range(TT):
                last = tr(BANK[7][:, t * P:(t + 1) * P], g_alt[1][:, t * P:(t + 1) * P], ident[:])
            last.then_inc(vT_mm, 1)

        with pe.Fori(0, 2) as i:
            for p in range(2):
                pe.wait_ge(xn_ok[p], 4 * (i + 1))
                for kt in range(KT):
                    pe.wait_ge(xl_ok[1 - p], CREDIT + 4 * (i + p - 1) + kt + 1)
                    for t in range(TT):
                        last = tr(BANK[kt][:, t * P:(t + 1) * P], xn[p][:, t, kt * P:(kt + 1) * P], ident[:])
                    last.then_inc(xT_ok[p], 1)
            for p in range(2):
                b = 2 * i + p
                pe.wait_ge(xl_ok[p], CREDIT + 4 * (i + 1))
                for m in range(MT):
                    pe.wait_ge(yq_ok, CREDIT + MT * b + m - 2)
                    w = slice(m * P, (m + 1) * P)
                    for kt in range(KT):
                        mm(BANK[4 + m % 3], signs[:, kt, w], xh[p][:, kt, :], start=(kt == 0), stop=False)
                        last = mm(BANK[4 + m % 3], signs[:, kt, w], xl[p][:, kt, :], start=False, stop=(kt == KT - 1))
                    last.then_inc(q_mm, 1)
                    if p == 1 and m == 1:
                        transpose_values_in(b - 1)
            pe.wait_ge(v_ok, 2 * i + 1)
            transpose_values_in(2 * i + 1)

        pe.wait_ge(v_ok, BATCH)
        pe.wait_ge(slot_init, 14)

        def scores(i, nn, tiles=(0, 1)):
            rel, j, half_tile = nn // 8, nn % 8 // 2, nn % 2
            s = rel % 4
            if nn % 8 == 0 and tiles[0] == 0:
                if isinstance(i, int) and 4 * i + rel < 3:
                    pe.wait_ge(first_in[s], 48)
                else:
                    pe.wait_ge(slot_in[s], 48 * (i + rel // 4 + 1))
                positive(pe, cleared, 4 * i + rel - 3)
            if tiles[0] == 0:
                positive(pe, s_max, 32 * i + nn - 1)
            for a in tiles:
                q = 2 * half_tile + a
                last = mm(BANK[q], q_slot[s][:, j, q * P:(q + 1) * P], k_slot[s][:], start=True, stop=True)
            if tiles[-1] == 1:
                last.then_inc(s_mm, 1)

        def transpose_maxima(g, s):
            pe.wait_ge(s_max, 8 * g + 8)
            positive(pe, sh_lo, g)
            tr(BANK[7][0:REP * TT, 0:P], nmx[s % 2][:], ident[:]).then_inc(mT_ok, 1)

        def shifted_scores(i, s, kt, j):
            g = 4 * i + s
            if kt == 0 and j == 0:
                pe.wait_ge(shift_in[s], 32 * (i + 1))
            positive(pe, exp_ok, 16 * g + 4 * kt + j - 1)
            mm(BANK[4 + j % 2], k_slot[s][:, kt * P:(kt + 1) * P], q_slot[s][:, j, :],
               start=True, stop=True).then_inc(t_mm, 1)

        def weigh_values(g, s, kt):
            pe.wait_ge(exp_ok, 16 * g + 4 * kt + 4)
            if kt == 0:
                pe.wait_ge(vs_ok, g + 1)
                positive(pe, u_ok, g)
            for j in range(REP):
                last = mm(psum[32 * j:32 * j + 32, 6, :], v_slot[s % 2][:, kt, :], probs[kt][:, j, :],
                          start=(kt == 0), stop=(kt == TT - 1))
            last.then_inc(pv_mm, 1)

        def project(b, t):
            if t == 0:
                pe.wait_ge(al_ok, 4 * (b + 1))
                positive(pe, fxl_ok, 4 * b)
            if t >= 2 and not isinstance(b, int):
                pe.wait_ge(oy_ok, 4 * b + t - 1)
            for kt in range(KT):
                mm(BANK[att_bank(b, t)], ah[:, kt, t * P:(t + 1) * P], signs_o[:, kt, :], start=(kt == 0), stop=False)
                last = mm(BANK[att_bank(b, t)], al[:, kt, t * P:(t + 1) * P], signs_o[:, kt, :],
                          start=False, stop=(kt == KT - 1))
            last.then_inc(o_mm, 1)

        def transpose_norm(b, kt):
            if kt == 0:
                pe.wait_ge(xn2_ok, 4 * (b + 1))
                pe.wait_ge(oy_ok, 4 * (b + 1))
            if kt >= 2:
                if isinstance(b, int):
                    pe.wait_ge(fxl_ok, kt - 1)
                else:
                    pe.wait_ge((silu_ok, h_ok)[kt - 2], CREDIT + IT * b)
            for t in range(TT):
                last = tr(BANK[norm_bank(b, kt)][:, t * P:(t + 1) * P], an[:, t, kt * P:(kt + 1) * P], ident[:])
            last.then_inc(x2T_mm, 1)

        def pe_steps(i, first=False, last=False):
            for s in range(4):
                g = 4 * i + s
                for kt in range(TT):
                    nn = 8 * s + 2 * kt + S_AHEAD
                    further = not (last and nn >= 32)
                    shifted_scores(i, s, kt, 0)
                    if further:
                        scores(i, nn, (0,))
                    shifted_scores(i, s, kt, 1)
                    if further:
                        scores(i, nn, (1,))
                        scores(i, nn + 1, (0,))
                    shifted_scores(i, s, kt, 2)
                    if further:
                        scores(i, nn + 1, (1,))
                    shifted_scores(i, s, kt, 3)
                    if kt > 0:
                        weigh_values(g, s, kt - 1)
                    elif not (first and s == 0):
                        weigh_values(g - 1, s + 3, TT - 1)
                    if kt == 1 and not (last and s == 3):
                        transpose_maxima(g + 1, s + 1)
                    if last and (s, kt) == MEANS_STEP:
                        pe.wait_ge(dtot_ok, 1)
                        pe.wait_ge(s_max, S_USES)
                        mm(BANK[MEAN_BANK][:, 0:3], ones[:], dtot[:], start=True, stop=True).then_inc(ctot_mm, 1)
                        pe.wait_ge(coeff_ok, 1)
                    if last and (s, kt) in PROJECT_STEPS:
                        project(0, PROJECT_STEPS.index((s, kt)))

        for nn in range(S_AHEAD):
            scores(0, nn)
            if nn == 8:
                transpose_maxima(0, 0)
        pe_steps(0, first=True)
        with pe.Fori(1, GROUPS // 4 - 1) as i:
            pe_steps(i)
        pe_steps(GROUPS // 4 - 1, last=True)
        weigh_values(LAST_G, 3, TT - 1)
        pe.wait_ge(u_ok, GROUPS)
        for e in range(IT):
            for k in range(3):
                pe.wait_ge(w_ok, 3 * e + k + 1)
                if e == 1 and k == 0:
                    pe.wait_ge(oy_ok, TT)
                if e >= 2:
                    pe.wait_ge(wT_ok, 3 * (e - 2) + k + 1)
                for t in range(TT):
                    last = tr(BANK[3 * (e % 2) + k][:, t * P:(t + 1) * P], stage[e % RING][:, k, t * P:(t + 1) * P], ident[:])
                last.then_inc(wT_mm, 1)
            if e + 1 in NORM_TILES:
                n = 2 * NORM_TILES.index(e + 1)
                transpose_norm(0, n)
                transpose_norm(0, n + 1)
        pe.wait_ge(wT_ok, 3 * IT)

        def three(o, lhs_hi, lhs_lo, rhs_hi, rhs_lo, first, final):
            mm(o, lhs_hi, rhs_hi, start=first, stop=False)
            mm(o, lhs_hi, rhs_lo, start=False, stop=False)
            return mm(o, lhs_lo, rhs_hi, start=False, stop=final)

        def gate_up(n, p, start=None):
            for k, (bank, used, done) in enumerate(((GATE, silu_ok, g_mm), (UP, h_ok, u_mm))):
                pe.wait_ge(wl_ok, 2 * n + k + 1)
                pe.wait_ge(used, CREDIT + n)
                for kt in range(KT):
                    c = slice(kt * P, (kt + 1) * P)
                    last = three(BANK[bank], wh[p][:, k, c], wl[p][:, k, c], fxh[:, kt, :], fxl[:, kt, :],
                                 kt == 0, kt == KT - 1)
                last.then_inc(done, 1)

        def down(n, p, first, final):
            pe.wait_ge(dl_ok, n + 1)
            pe.wait_ge(hl_ok, CREDIT + n + 1)
            for t in range(TT):
                c = slice(t * P, (t + 1) * P)
                last = three(BANK[DOWN + t], hh[p][:, c], hl[p][:, c], dh[p][:], dl[p][:], first, final)
            last.then_inc(d_mm, 1)

        with pe.Fori(0, BATCH - 1) as b:
            pe.wait_ge(fxl_ok, 4 * (b + 1))
            for e in range(IT):
                gate_up(IT * b + e, e % 2)
                if e == 1:
                    pe.wait_ge(res_ok, CREDIT + 4 * b)
                if e > 0:
                    down(IT * b + e - 1, (e - 1) % 2, e == 1, False)
                if LAG + KT <= e < LAG + KT + TT:
                    project(b + 1, e - LAG - KT)
            for kt in range(KT):
                transpose_norm(b + 1, kt)
            down(IT * (b + 1) - 1, 1, False, True)
        n = IT * (BATCH - 1)
        pe.wait_ge(fxl_ok, 4 * BATCH)
        gate_up(n, 0)
        gate_up(n + 1, 1)
        pe.wait_ge(res_ok, CREDIT + 4 * (BATCH - 1))
        down(n, 0, True, False)
        with pe.Fori(1, IT // 2) as i:
            for p in range(2):
                gate_up(n + 2 * i + p, p)
                down(n + 2 * i + p - 1, 1 - p, False, False)
        down(IT * BATCH - 1, 1, False, True)

    ctx.close()


_INS = ["L0_attn_hidden_states", "L0_attn_q_weight", "L0_attn_q_scale", "L0_attn_k_weight", "L0_attn_k_scale",
        "L0_attn_v_weight", "L0_attn_v_scale", "L0_attn_o_weight", "L0_attn_o_scale",
        "L0_ffn_w1", "L0_ffn_mean_w1", "L0_ffn_w2", "L0_ffn_mean_w2", "L0_ffn_w3", "L0_ffn_mean_w3"]
_OUTS = [((BATCH, SEQ, HID), "float32")]


def kernel(**inputs):
    import numpy as _np
    import concourse.bacc as _bacc
    from concourse import mybir as _mybir
    from concourse.bass_utils import run_bass_kernel_spmd as _run

    nc = _bacc.Bacc("TRN2", target_bir_lowering=False, num_devices=1)
    arrays, args = {}, []
    for name in _INS:
        a = _np.ascontiguousarray(inputs[name])
        arrays[f"in_{name}_dram"] = a
        args.append(nc.dram_tensor(f"in_{name}_dram", a.shape, _mybir.dt.from_np(a.dtype), kind="ExternalInput").ap())
    for i, (shape, dtype) in enumerate(_OUTS):
        dt = _mybir.dt.from_np(_np.dtype(dtype))
        args.append(nc.dram_tensor(f"out_{i}_dram", shape, dt, kind="ExternalOutput").ap())
    decoder_layer(nc, *args)
    r = _run(nc, [arrays], core_ids=[0])
    return r.results[0]["out_0_dram"]
```
